# Optimizing a Trainium2 kernel written in Bass

```python
import numpy as np
import jax
import jax.numpy as jnp

def _softmax(x, axis=-1):
    return jax.nn.softmax(x, axis=axis)
def _gelu(x):
    return jax.nn.gelu(x, approximate=True)
def _silu(x):
    return jax.nn.silu(x)
def _sigmoid(x):
    return jax.nn.sigmoid(x)
def _layernorm(x, axis=-1, eps=1e-5):
    m = jnp.mean(x, axis=axis, keepdims=True)
    v = jnp.var(x, axis=axis, keepdims=True)
    return (x - m) / jnp.sqrt(v + eps)
def _scatter_add(tgt, idx, src, axis=0):
    return tgt.at[idx].add(src)
def _segment_sum(src, seg, n):
    return jax.ops.segment_sum(src, seg, n)

kernel_name = 'mk_conv_preact_d4_conv_nhwc192_1e7ddb'

def setup_inputs(seed: int = 0):
    np.random.seed(seed)
    _w = jnp.asarray
    def _rec_inputs():
        import jax
        import jax.numpy as jnp
        _gk = jax.random.key(seed)
        x = -0.0005963 + 1.001 * jax.random.normal(jax.random.fold_in(_gk, 1), (4, 64, 64, 192), jnp.float32)
        return x
    x = _rec_inputs()
    def _L0_conv_setup():
        import jax, jax.numpy as jnp
        import numpy as np
        D_MODEL = 192
        D_STATE = 16
        D_INNER = 384
        DT_RANK = 12
        K = 4
        B_, H_, W_ = (4, 64, 64)
        EPS = 1e-06

        def _selective_scan(u, delta, A, Bs, Cs, Ds, delta_bias):
            Bb, KD, L = u.shape
            N = A.shape[1]
            D = KD // K
            delta = jax.nn.softplus(delta + delta_bias[None, :, None])
            u_k = u.reshape(Bb, K, D, L)
            d_k = delta.reshape(Bb, K, D, L)
            A_k = A.reshape(K, D, N)

            def step(h, inp):
                dt, ut, bt, ct = inp
                dA = jnp.exp(dt[..., None] * A_k[None])
                dBu = dt[..., None] * bt[:, :, None, :] * ut[..., None]
                h = dA * h + dBu
                y = jnp.einsum('bkdn,bkn->bkd', h, ct)
                return (h, y)
            h0 = jnp.zeros((Bb, K, D, N), u.dtype)
            inps = (jnp.moveaxis(d_k, -1, 0), jnp.moveaxis(u_k, -1, 0), jnp.moveaxis(Bs, -1, 0), jnp.moveaxis(Cs, -1, 0))
            _, ys = jax.lax.scan(step, h0, inps)
            y = jnp.moveaxis(ys, 0, -1).reshape(Bb, KD, L)
            return y + u * Ds[None, :, None]
        key = jax.random.key(seed)
        ks = jax.random.split(key, 7)
        x = jax.random.normal(ks[0], (B_, H_, W_, D_MODEL), jnp.float32)
        in_proj_weight = jax.random.normal(ks[1], (2 * D_INNER, D_MODEL), jnp.float32) * D_MODEL ** (-0.5)
        out_proj_weight = jax.random.normal(ks[2], (D_MODEL, D_INNER), jnp.float32) * D_INNER ** (-0.5)
        x_proj_weight = jax.random.normal(ks[3], (K, DT_RANK + 2 * D_STATE, D_INNER), jnp.float32) * 0.02
        dt_projs_weight = jax.random.normal(ks[4], (K, D_INNER, DT_RANK), jnp.float32) * DT_RANK ** (-0.5)
        dt = jnp.exp(jax.random.uniform(ks[5], (K, D_INNER)) * (np.log(0.1) - np.log(0.001)) + np.log(0.001))
        dt = jnp.clip(dt, 0.0001, None)
        dt_projs_bias = dt + jnp.log(-jnp.expm1(-dt))
        A_logs = jnp.log(jnp.tile(jnp.arange(1, D_STATE + 1, dtype=jnp.float32)[None, :], (K * D_INNER, 1)))
        Ds = jnp.ones((K * D_INNER,), jnp.float32)
        out_norm_weight = jnp.ones((D_INNER,), jnp.float32)
        out_norm_bias = jnp.zeros((D_INNER,), jnp.float32)
        return dict(x=x, in_proj_weight=in_proj_weight, out_proj_weight=out_proj_weight, x_proj_weight=x_proj_weight, dt_projs_weight=dt_projs_weight, dt_projs_bias=dt_projs_bias, A_logs=A_logs, Ds=Ds, out_norm_weight=out_norm_weight, out_norm_bias=out_norm_bias)
    _L0_conv_all = _L0_conv_setup()
    _L0_conv_in = {k: v for k, v in _L0_conv_all.items() if k in ('in_proj_weight', 'out_proj_weight', 'x_proj_weight', 'dt_projs_weight', 'dt_projs_bias', 'A_logs', 'Ds', 'out_norm_weight', 'out_norm_bias', )}
    del _L0_conv_all

    def _L1_conv_setup():
        import jax, jax.numpy as jnp
        import numpy as np
        B, H, W = (8, 48, 48)
        D_MODEL, D_STATE, SSM_RATIO, K = (192, 16, 2.0, 4)
        D_INNER = int(SSM_RATIO * D_MODEL)
        DT_RANK = int(np.ceil(D_MODEL / 16))
        EPS = 1e-06

        def _selective_scan(u, dt, A, Bs, Cs):
            u_t = jnp.moveaxis(u, -1, 0)
            dt_t = jnp.moveaxis(dt, -1, 0)
            B_t = jnp.moveaxis(Bs, -1, 0)
            C_t = jnp.moveaxis(Cs, -1, 0)
            b = u.shape[0]
            h0 = jnp.zeros((b, K, D_INNER, D_STATE), jnp.float32)

            def step(h, inp):
                ut, dtt, bt, ct = inp
                dA = jnp.exp(dtt[..., None] * A)
                h = dA * h + (dtt * ut)[..., None] * bt[:, :, None, :]
                y = jnp.einsum('bkdn,bkn->bkd', h, ct)
                return (h, y)
            _, ys = jax.lax.scan(step, h0, (u_t, dt_t, B_t, C_t))
            return jnp.moveaxis(ys, 0, -1)
        key = jax.random.key(seed)
        ks = jax.random.split(key, 12)
        s = 0.02
        inp = {'x': jax.random.normal(ks[0], (B, H, W, D_MODEL), jnp.float32), 'in_proj_w': s * jax.random.normal(ks[1], (2 * D_INNER, D_MODEL), jnp.float32), 'conv_w': s * jax.random.normal(ks[2], (D_INNER, 1, 3, 3), jnp.float32), 'conv_b': jnp.zeros((D_INNER,), jnp.float32), 'x_proj_w': s * jax.random.normal(ks[3], (K, DT_RANK + 2 * D_STATE, D_INNER), jnp.float32), 'dt_w': s * jax.random.normal(ks[4], (K, D_INNER, DT_RANK), jnp.float32), 'dt_bias': 0.05 * jax.random.normal(ks[5], (K, D_INNER), jnp.float32), 'A_logs': jnp.log(jnp.broadcast_to(jnp.arange(1, D_STATE + 1, dtype=jnp.float32), (K * D_INNER, D_STATE)).copy()), 'Ds': jnp.ones((K * D_INNER,), jnp.float32), 'ln_w': jnp.ones((D_INNER,), jnp.float32), 'ln_b': jnp.zeros((D_INNER,), jnp.float32), 'out_proj_w': s * jax.random.normal(ks[6], (D_MODEL, D_INNER), jnp.float32)}
        return inp
    _L1_conv_all = _L1_conv_setup()
    _L1_conv_in = {k: v for k, v in _L1_conv_all.items() if k in ('in_proj_w', 'conv_w', 'conv_b', 'x_proj_w', 'dt_w', 'dt_bias', 'A_logs', 'Ds', 'ln_w', 'ln_b', 'out_proj_w', )}
    del _L1_conv_all

    def _L2_conv_setup():
        import jax, jax.numpy as jnp
        import numpy as np
        B0, H0, W0 = (4, 64, 64)
        D_MODEL, D_STATE, D_CONV, EXPAND = (192, 16, 3, 2.0)
        D_INNER = int(EXPAND * D_MODEL)
        DT_RANK = (D_MODEL + 1) // 2
        K = 4
        EPS = 1e-05

        def _selective_scan(u, delta, A, Bs, Cs, Dp):
            b = u.shape[0]
            uT = jnp.transpose(u, (3, 0, 1, 2))
            dT = jnp.transpose(delta, (3, 0, 1, 2))
            BT = jnp.transpose(Bs, (3, 0, 1, 2))
            CT = jnp.transpose(Cs, (3, 0, 1, 2))
            h0 = jnp.zeros((b, K, D_INNER, D_STATE), u.dtype)

            def step(h, inp):
                dl, ul, Bl, Cl = inp
                dA = jnp.exp(dl[..., None] * A)
                h = dA * h + (dl * ul)[..., None] * Bl[:, :, None, :]
                y = jnp.einsum('bkdn,bkn->bkd', h, Cl)
                return (h, y)
            _, ys = jax.lax.scan(step, h0, (dT, uT, BT, CT))
            y = jnp.transpose(ys, (1, 2, 3, 0))
            return y + u * Dp[None, :, :, None]
        key = jax.random.key(seed)
        ks = jax.random.split(key, 10)
        x = jax.random.normal(ks[0], (B0, H0, W0, D_MODEL), dtype=jnp.float32)
        in_proj_w = jax.random.normal(ks[1], (2 * D_INNER, D_MODEL), jnp.float32) * D_MODEL ** (-0.5)
        conv_w = jax.random.normal(ks[2], (D_INNER, 1, D_CONV, D_CONV), jnp.float32) * (1.0 / D_CONV)
        conv_b = jnp.zeros((D_INNER,), jnp.float32)
        x_proj_weight = jax.random.normal(ks[3], (K, DT_RANK + 2 * D_STATE, D_INNER), jnp.float32) * D_INNER ** (-0.5)
        dt_init_std = DT_RANK ** (-0.5)
        dt_projs_weight = jax.random.uniform(ks[4], (K, D_INNER, DT_RANK), jnp.float32, -dt_init_std, dt_init_std)
        u = jax.random.uniform(ks[5], (K, D_INNER), jnp.float32)
        dt = jnp.exp(u * (np.log(0.1) - np.log(0.001)) + np.log(0.001))
        dt = jnp.clip(dt, 0.0001, None)
        dt_projs_bias = dt + jnp.log(-jnp.expm1(-dt))
        A_logs = jnp.log(jnp.tile(jnp.arange(1, D_STATE + 1, dtype=jnp.float32)[None, :], (K * D_INNER, 1)))
        Ds = jnp.ones((K * D_INNER,), jnp.float32)
        ln_gamma = jnp.ones((D_INNER,), jnp.float32)
        ln_beta = jnp.zeros((D_INNER,), jnp.float32)
        out_proj_w = jax.random.normal(ks[6], (D_MODEL, D_INNER), jnp.float32) * D_INNER ** (-0.5)
        return dict(x=x, in_proj_w=in_proj_w, conv_w=conv_w, conv_b=conv_b, x_proj_weight=x_proj_weight, dt_projs_weight=dt_projs_weight, dt_projs_bias=dt_projs_bias, A_logs=A_logs, Ds=Ds, ln_gamma=ln_gamma, ln_beta=ln_beta, out_proj_w=out_proj_w)
    _L2_conv_all = _L2_conv_setup()
    _L2_conv_in = {k: v for k, v in _L2_conv_all.items() if k in ('in_proj_w', 'conv_w', 'conv_b', 'x_proj_weight', 'dt_projs_weight', 'dt_projs_bias', 'A_logs', 'Ds', 'ln_gamma', 'ln_beta', 'out_proj_w', )}
    del _L2_conv_all

    def _L3_conv_setup():
        import jax, jax.numpy as jnp
        import numpy as np
        D_MODEL = 192
        D_STATE = 16
        EXPAND = 2
        D_INNER = EXPAND * D_MODEL
        DT_RANK = 12
        K = 4
        LN_EPS = 1e-05

        def _silu(v):
            return v * jax.nn.sigmoid(v)

        def _cross_scan(xh):
            B, H, W, C = xh.shape
            s1 = xh.reshape(B, H * W, C)
            s2 = xh[:, :, ::-1, :].reshape(B, H * W, C)
            s3 = xh[:, ::-1, :, :].reshape(B, H * W, C)
            s4 = xh[:, ::-1, ::-1, :].reshape(B, H * W, C)
            return jnp.stack([s1, s2, s3, s4], axis=1)

        def _merge_scans(y_scans, H, W):
            B, Kk, L, C = y_scans.shape
            y = y_scans.reshape(B, Kk, H, W, C)
            y1 = y[:, 0]
            y2 = y[:, 1][:, :, ::-1, :]
            y3 = y[:, 2][:, ::-1, :, :]
            y4 = y[:, 3][:, ::-1, ::-1, :]
            return (y1 + y2 + y3 + y4) * 0.25
        key = jax.random.key(seed)
        ks = jax.random.split(key, 12)
        B, H, W = (8, 64, 64)
        x = jax.random.normal(ks[0], (B, H, W, D_MODEL), dtype=jnp.float32)
        in_proj_w = jax.random.normal(ks[1], (2 * D_INNER, D_MODEL), dtype=jnp.float32) * 0.02
        conv_w = jax.random.normal(ks[2], (3, 3, 1, D_INNER), dtype=jnp.float32) * 0.05
        conv_b = jnp.zeros((D_INNER,), dtype=jnp.float32)
        x_proj_weight = jax.random.normal(ks[3], (K, DT_RANK + 2 * D_STATE, D_INNER), dtype=jnp.float32) * 0.02
        dt_projs_weight = jax.random.normal(ks[4], (K, D_INNER, DT_RANK), dtype=jnp.float32) * 0.02
        dt = jnp.exp(jax.random.uniform(ks[5], (K, D_INNER)) * (np.log(0.1) - np.log(0.001)) + np.log(0.001))
        dt = jnp.clip(dt, 0.0001, None)
        dt_projs_bias = dt + jnp.log(-jnp.expm1(-dt))
        A_logs = jnp.log(jnp.abs(jax.random.normal(ks[6], (D_INNER * K, D_STATE), dtype=jnp.float32)) + 1e-06)
        Ds = jnp.ones((D_INNER * K,), dtype=jnp.float32)
        ln_gamma = jnp.ones((D_INNER,), dtype=jnp.float32)
        ln_beta = jnp.zeros((D_INNER,), dtype=jnp.float32)
        out_proj_w = jax.random.normal(ks[7], (D_MODEL, D_INNER), dtype=jnp.float32) * 0.02
        return dict(x=x, in_proj_w=in_proj_w, conv_w=conv_w, conv_b=conv_b, x_proj_weight=x_proj_weight, dt_projs_weight=dt_projs_weight, dt_projs_bias=dt_projs_bias, A_logs=A_logs, Ds=Ds, ln_gamma=ln_gamma, ln_beta=ln_beta, out_proj_w=out_proj_w)
    _L3_conv_all = _L3_conv_setup()
    _L3_conv_in = {k: v for k, v in _L3_conv_all.items() if k in ('in_proj_w', 'conv_w', 'conv_b', 'x_proj_weight', 'dt_projs_weight', 'dt_projs_bias', 'A_logs', 'Ds', 'ln_gamma', 'ln_beta', 'out_proj_w', )}
    del _L3_conv_all

    return {
        "x": x,
        "L0_conv_in_proj_weight": _L0_conv_in["in_proj_weight"],
        "L0_conv_out_proj_weight": _L0_conv_in["out_proj_weight"],
        "L0_conv_x_proj_weight": _L0_conv_in["x_proj_weight"],
        "L0_conv_dt_projs_weight": _L0_conv_in["dt_projs_weight"],
        "L0_conv_dt_projs_bias": _L0_conv_in["dt_projs_bias"],
        "L0_conv_A_logs": _L0_conv_in["A_logs"],
        "L0_conv_Ds": _L0_conv_in["Ds"],
        "L0_conv_out_norm_weight": _L0_conv_in["out_norm_weight"],
        "L0_conv_out_norm_bias": _L0_conv_in["out_norm_bias"],
        "L1_conv_in_proj_w": _L1_conv_in["in_proj_w"],
        "L1_conv_conv_w": _L1_conv_in["conv_w"],
        "L1_conv_conv_b": _L1_conv_in["conv_b"],
        "L1_conv_x_proj_w": _L1_conv_in["x_proj_w"],
        "L1_conv_dt_w": _L1_conv_in["dt_w"],
        "L1_conv_dt_bias": _L1_conv_in["dt_bias"],
        "L1_conv_A_logs": _L1_conv_in["A_logs"],
        "L1_conv_Ds": _L1_conv_in["Ds"],
        "L1_conv_ln_w": _L1_conv_in["ln_w"],
        "L1_conv_ln_b": _L1_conv_in["ln_b"],
        "L1_conv_out_proj_w": _L1_conv_in["out_proj_w"],
        "L2_conv_in_proj_w": _L2_conv_in["in_proj_w"],
        "L2_conv_conv_w": _L2_conv_in["conv_w"],
        "L2_conv_conv_b": _L2_conv_in["conv_b"],
        "L2_conv_x_proj_weight": _L2_conv_in["x_proj_weight"],
        "L2_conv_dt_projs_weight": _L2_conv_in["dt_projs_weight"],
        "L2_conv_dt_projs_bias": _L2_conv_in["dt_projs_bias"],
        "L2_conv_A_logs": _L2_conv_in["A_logs"],
        "L2_conv_Ds": _L2_conv_in["Ds"],
        "L2_conv_ln_gamma": _L2_conv_in["ln_gamma"],
        "L2_conv_ln_beta": _L2_conv_in["ln_beta"],
        "L2_conv_out_proj_w": _L2_conv_in["out_proj_w"],
        "L3_conv_in_proj_w": _L3_conv_in["in_proj_w"],
        "L3_conv_conv_w": _L3_conv_in["conv_w"],
        "L3_conv_conv_b": _L3_conv_in["conv_b"],
        "L3_conv_x_proj_weight": _L3_conv_in["x_proj_weight"],
        "L3_conv_dt_projs_weight": _L3_conv_in["dt_projs_weight"],
        "L3_conv_dt_projs_bias": _L3_conv_in["dt_projs_bias"],
        "L3_conv_A_logs": _L3_conv_in["A_logs"],
        "L3_conv_Ds": _L3_conv_in["Ds"],
        "L3_conv_ln_gamma": _L3_conv_in["ln_gamma"],
        "L3_conv_ln_beta": _L3_conv_in["ln_beta"],
        "L3_conv_out_proj_w": _L3_conv_in["out_proj_w"],
    }

def reference(x, L0_conv_in_proj_weight, L0_conv_out_proj_weight, L0_conv_x_proj_weight, L0_conv_dt_projs_weight, L0_conv_dt_projs_bias, L0_conv_A_logs, L0_conv_Ds, L0_conv_out_norm_weight, L0_conv_out_norm_bias, L1_conv_in_proj_w, L1_conv_conv_w, L1_conv_conv_b, L1_conv_x_proj_w, L1_conv_dt_w, L1_conv_dt_bias, L1_conv_A_logs, L1_conv_Ds, L1_conv_ln_w, L1_conv_ln_b, L1_conv_out_proj_w, L2_conv_in_proj_w, L2_conv_conv_w, L2_conv_conv_b, L2_conv_x_proj_weight, L2_conv_dt_projs_weight, L2_conv_dt_projs_bias, L2_conv_A_logs, L2_conv_Ds, L2_conv_ln_gamma, L2_conv_ln_beta, L2_conv_out_proj_w, L3_conv_in_proj_w, L3_conv_conv_w, L3_conv_conv_b, L3_conv_x_proj_weight, L3_conv_dt_projs_weight, L3_conv_dt_projs_bias, L3_conv_A_logs, L3_conv_Ds, L3_conv_ln_gamma, L3_conv_ln_beta, L3_conv_out_proj_w):
    import jax
    import jax.numpy as jnp
    def _L0_conv_ref(x, in_proj_weight, out_proj_weight, x_proj_weight, dt_projs_weight, dt_projs_bias, A_logs, Ds, out_norm_weight, out_norm_bias):
        import jax, jax.numpy as jnp
        import numpy as np
        D_MODEL = 192
        D_STATE = 16
        D_INNER = 384
        DT_RANK = 12
        K = 4
        B_, H_, W_ = (4, 64, 64)
        EPS = 1e-06

        def _selective_scan(u, delta, A, Bs, Cs, Ds, delta_bias):
            Bb, KD, L = u.shape
            N = A.shape[1]
            D = KD // K
            delta = jax.nn.softplus(delta + delta_bias[None, :, None])
            u_k = u.reshape(Bb, K, D, L)
            d_k = delta.reshape(Bb, K, D, L)
            A_k = A.reshape(K, D, N)

            def step(h, inp):
                dt, ut, bt, ct = inp
                dA = jnp.exp(dt[..., None] * A_k[None])
                dBu = dt[..., None] * bt[:, :, None, :] * ut[..., None]
                h = dA * h + dBu
                y = jnp.einsum('bkdn,bkn->bkd', h, ct)
                return (h, y)
            h0 = jnp.zeros((Bb, K, D, N), u.dtype)
            inps = (jnp.moveaxis(d_k, -1, 0), jnp.moveaxis(u_k, -1, 0), jnp.moveaxis(Bs, -1, 0), jnp.moveaxis(Cs, -1, 0))
            _, ys = jax.lax.scan(step, h0, inps)
            y = jnp.moveaxis(ys, 0, -1).reshape(Bb, KD, L)
            return y + u * Ds[None, :, None]
        Bb, H, W, C = x.shape
        L = H * W
        xz = jnp.einsum('bhwc,ec->bhwe', x, in_proj_weight)
        xin, z = jnp.split(xz, 2, axis=-1)
        xc = jnp.transpose(xin, (0, 3, 1, 2))
        x_hw = xc.reshape(Bb, D_INNER, L)
        x_wh = jnp.transpose(xc, (0, 1, 3, 2)).reshape(Bb, D_INNER, L)
        x_hwwh = jnp.stack([x_hw, x_wh], axis=1)
        xs = jnp.concatenate([x_hwwh, jnp.flip(x_hwwh, axis=-1)], axis=1)
        x_dbl = jnp.einsum('bkdl,kcd->bkcl', xs, x_proj_weight)
        dts = x_dbl[:, :, :DT_RANK]
        Bs = x_dbl[:, :, DT_RANK:DT_RANK + D_STATE]
        Cs = x_dbl[:, :, DT_RANK + D_STATE:]
        dts = jnp.einsum('bkrl,kdr->bkdl', dts, dt_projs_weight)
        As = -jnp.exp(A_logs)
        out_y = _selective_scan(xs.reshape(Bb, -1, L), dts.reshape(Bb, -1, L), As, Bs, Cs, Ds, dt_projs_bias.reshape(-1)).reshape(Bb, K, D_INNER, L)
        inv_y = jnp.flip(out_y[:, 2:4], axis=-1)
        wh_y = jnp.transpose(out_y[:, 1].reshape(Bb, D_INNER, W, H), (0, 1, 3, 2)).reshape(Bb, D_INNER, L)
        invwh_y = jnp.transpose(inv_y[:, 1].reshape(Bb, D_INNER, W, H), (0, 1, 3, 2)).reshape(Bb, D_INNER, L)
        y = out_y[:, 0] + inv_y[:, 0] + wh_y + invwh_y
        y4 = y.reshape(Bb, D_INNER, H, W)
        mu = y4.mean(1, keepdims=True)
        var = ((y4 - mu) ** 2).mean(1, keepdims=True)
        y4 = (y4 - mu) / jnp.sqrt(var + EPS)
        y4 = out_norm_weight[None, :, None, None] * y4 + out_norm_bias[None, :, None, None]
        y = jnp.transpose(y4, (0, 2, 3, 1))
        y = y * jax.nn.silu(z)
        return jnp.einsum('bhwd,cd->bhwc', y, out_proj_weight)

    def _L1_conv_ref(x, in_proj_w, conv_w, conv_b, x_proj_w, dt_w, dt_bias, A_logs, Ds, ln_w, ln_b, out_proj_w):
        import jax, jax.numpy as jnp
        import numpy as np
        B, H, W = (8, 48, 48)
        D_MODEL, D_STATE, SSM_RATIO, K = (192, 16, 2.0, 4)
        D_INNER = int(SSM_RATIO * D_MODEL)
        DT_RANK = int(np.ceil(D_MODEL / 16))
        EPS = 1e-06

        def _selective_scan(u, dt, A, Bs, Cs):
            u_t = jnp.moveaxis(u, -1, 0)
            dt_t = jnp.moveaxis(dt, -1, 0)
            B_t = jnp.moveaxis(Bs, -1, 0)
            C_t = jnp.moveaxis(Cs, -1, 0)
            b = u.shape[0]
            h0 = jnp.zeros((b, K, D_INNER, D_STATE), jnp.float32)

            def step(h, inp):
                ut, dtt, bt, ct = inp
                dA = jnp.exp(dtt[..., None] * A)
                h = dA * h + (dtt * ut)[..., None] * bt[:, :, None, :]
                y = jnp.einsum('bkdn,bkn->bkd', h, ct)
                return (h, y)
            _, ys = jax.lax.scan(step, h0, (u_t, dt_t, B_t, C_t))
            return jnp.moveaxis(ys, 0, -1)
        b, h, w, _ = x.shape
        L = h * w
        xz = jnp.einsum('bhwc,oc->bhwo', x, in_proj_w)
        xi, z = jnp.split(xz, 2, axis=-1)
        z = jax.nn.silu(z)
        xi = jnp.transpose(xi, (0, 3, 1, 2))
        xi = jax.lax.conv_general_dilated(xi, conv_w, window_strides=(1, 1), padding='SAME', feature_group_count=D_INNER, dimension_numbers=('NCHW', 'OIHW', 'NCHW')) + conv_b[None, :, None, None]
        xi = jax.nn.silu(xi)
        xr = xi.reshape(b, D_INNER, L)
        xc = jnp.transpose(xi, (0, 1, 3, 2)).reshape(b, D_INNER, L)
        xs = jnp.stack([xr, xc, jnp.flip(xr, -1), jnp.flip(xc, -1)], axis=1)
        x_dbl = jnp.einsum('bkdl,kcd->bkcl', xs, x_proj_w)
        dts = x_dbl[:, :, :DT_RANK]
        Bs = x_dbl[:, :, DT_RANK:DT_RANK + D_STATE]
        Cs = x_dbl[:, :, DT_RANK + D_STATE:]
        dts = jnp.einsum('bkrl,kdr->bkdl', dts, dt_w)
        A = -jnp.exp(A_logs.astype(jnp.float32)).reshape(K, D_INNER, D_STATE)
        dt = jax.nn.softplus(dts + dt_bias[None, :, :, None])
        ys = _selective_scan(xs.astype(jnp.float32), dt, A, Bs.astype(jnp.float32), Cs.astype(jnp.float32))
        ys = ys + Ds.reshape(1, K, D_INNER, 1) * xs

        def col2row(t):
            return jnp.transpose(t.reshape(b, D_INNER, w, h), (0, 1, 3, 2)).reshape(b, D_INNER, L)
        y = ys[:, 0] + col2row(ys[:, 1]) + jnp.flip(ys[:, 2], -1) + col2row(jnp.flip(ys[:, 3], -1))
        y = jnp.transpose(y.reshape(b, D_INNER, h, w), (0, 2, 3, 1))
        mu = y.mean(-1, keepdims=True)
        var = ((y - mu) ** 2).mean(-1, keepdims=True)
        y = (y - mu) / jnp.sqrt(var + EPS) * ln_w + ln_b
        y = y * z
        out = jnp.einsum('bhwd,od->bhwo', y, out_proj_w)
        return out.astype(x.dtype)

    def _L2_conv_ref(x, in_proj_w, conv_w, conv_b, x_proj_weight, dt_projs_weight, dt_projs_bias, A_logs, Ds, ln_gamma, ln_beta, out_proj_w):
        import jax, jax.numpy as jnp
        import numpy as np
        B0, H0, W0 = (4, 64, 64)
        D_MODEL, D_STATE, D_CONV, EXPAND = (192, 16, 3, 2.0)
        D_INNER = int(EXPAND * D_MODEL)
        DT_RANK = (D_MODEL + 1) // 2
        K = 4
        EPS = 1e-05

        def _selective_scan(u, delta, A, Bs, Cs, Dp):
            b = u.shape[0]
            uT = jnp.transpose(u, (3, 0, 1, 2))
            dT = jnp.transpose(delta, (3, 0, 1, 2))
            BT = jnp.transpose(Bs, (3, 0, 1, 2))
            CT = jnp.transpose(Cs, (3, 0, 1, 2))
            h0 = jnp.zeros((b, K, D_INNER, D_STATE), u.dtype)

            def step(h, inp):
                dl, ul, Bl, Cl = inp
                dA = jnp.exp(dl[..., None] * A)
                h = dA * h + (dl * ul)[..., None] * Bl[:, :, None, :]
                y = jnp.einsum('bkdn,bkn->bkd', h, Cl)
                return (h, y)
            _, ys = jax.lax.scan(step, h0, (dT, uT, BT, CT))
            y = jnp.transpose(ys, (1, 2, 3, 0))
            return y + u * Dp[None, :, :, None]
        B, H, W, C = x.shape
        L = H * W
        xz = jnp.einsum('bhwc,dc->bhwd', x, in_proj_w)
        xp, z = jnp.split(xz, 2, axis=-1)
        xc = jnp.transpose(xp, (0, 3, 1, 2))
        xc = jax.lax.conv_general_dilated(xc, conv_w, window_strides=(1, 1), padding='SAME', feature_group_count=D_INNER, dimension_numbers=('NCHW', 'OIHW', 'NCHW')) + conv_b[None, :, None, None]
        xc = jax.nn.silu(xc)
        x_flat = xc.reshape(B, D_INNER, L)
        x_wh = jnp.transpose(xc, (0, 1, 3, 2)).reshape(B, D_INNER, L)
        x_hwwh = jnp.stack([x_flat, x_wh], axis=1)
        xs = jnp.concatenate([x_hwwh, jnp.flip(x_hwwh, axis=-1)], axis=1)
        x_dbl = jnp.einsum('bkdl,kcd->bkcl', xs, x_proj_weight)
        dts = x_dbl[:, :, :DT_RANK]
        Bs = x_dbl[:, :, DT_RANK:DT_RANK + D_STATE]
        Cs = x_dbl[:, :, DT_RANK + D_STATE:]
        dts = jnp.einsum('bkrl,kdr->bkdl', dts, dt_projs_weight)
        delta = jax.nn.softplus(dts + dt_projs_bias[None, :, :, None])
        A = -jnp.exp(A_logs).reshape(K, D_INNER, D_STATE)
        Dp = Ds.reshape(K, D_INNER)
        out_y = _selective_scan(xs, delta, A, Bs, Cs, Dp)
        y1 = out_y[:, 0]
        inv_y = jnp.flip(out_y[:, 2:4], axis=-1)
        y2 = inv_y[:, 0]
        y3 = jnp.transpose(out_y[:, 1].reshape(B, D_INNER, W, H), (0, 1, 3, 2)).reshape(B, D_INNER, L)
        y4 = jnp.transpose(inv_y[:, 1].reshape(B, D_INNER, W, H), (0, 1, 3, 2)).reshape(B, D_INNER, L)
        y = y1 + y2 + y3 + y4
        y = jnp.transpose(y, (0, 2, 1)).reshape(B, H, W, D_INNER)
        mu = jnp.mean(y, axis=-1, keepdims=True)
        var = jnp.mean(jnp.square(y - mu), axis=-1, keepdims=True)
        y = (y - mu) * jax.lax.rsqrt(var + EPS) * ln_gamma + ln_beta
        y = y * jax.nn.silu(z)
        return jnp.einsum('bhwd,cd->bhwc', y, out_proj_w)

    def _L3_conv_ref(x, in_proj_w, conv_w, conv_b, x_proj_weight, dt_projs_weight, dt_projs_bias, A_logs, Ds, ln_gamma, ln_beta, out_proj_w):
        import jax, jax.numpy as jnp
        import numpy as np
        D_MODEL = 192
        D_STATE = 16
        EXPAND = 2
        D_INNER = EXPAND * D_MODEL
        DT_RANK = 12
        K = 4
        LN_EPS = 1e-05

        def _silu(v):
            return v * jax.nn.sigmoid(v)

        def _cross_scan(xh):
            B, H, W, C = xh.shape
            s1 = xh.reshape(B, H * W, C)
            s2 = xh[:, :, ::-1, :].reshape(B, H * W, C)
            s3 = xh[:, ::-1, :, :].reshape(B, H * W, C)
            s4 = xh[:, ::-1, ::-1, :].reshape(B, H * W, C)
            return jnp.stack([s1, s2, s3, s4], axis=1)

        def _merge_scans(y_scans, H, W):
            B, Kk, L, C = y_scans.shape
            y = y_scans.reshape(B, Kk, H, W, C)
            y1 = y[:, 0]
            y2 = y[:, 1][:, :, ::-1, :]
            y3 = y[:, 2][:, ::-1, :, :]
            y4 = y[:, 3][:, ::-1, ::-1, :]
            return (y1 + y2 + y3 + y4) * 0.25
        B, H, W, C = x.shape
        xz = jnp.einsum('bhwc,oc->bhwo', x, in_proj_w)
        xh, z = jnp.split(xz, 2, axis=-1)
        xh = jax.lax.conv_general_dilated(xh, conv_w, window_strides=(1, 1), padding='SAME', dimension_numbers=('NHWC', 'HWIO', 'NHWC'), feature_group_count=D_INNER) + conv_b
        xh = _silu(xh)
        x_scans = _cross_scan(xh)
        x_dbl = jnp.einsum('bkli,koi->bklo', x_scans, x_proj_weight)
        dt, B_param, C_param = jnp.split(x_dbl, [DT_RANK, DT_RANK + D_STATE], axis=-1)
        dt = jnp.einsum('bklr,kir->bkli', dt, dt_projs_weight) + dt_projs_bias[None, :, None, :]
        dt = jax.nn.softplus(dt)
        A = -jnp.exp(A_logs)
        D = Ds.reshape(D_INNER, K)
        y_scans = x_scans * D.T[None, :, None, :]
        y = _merge_scans(y_scans, H, W)
        y = y * _silu(z)
        mu = jnp.mean(y, axis=-1, keepdims=True)
        var = jnp.mean(jnp.square(y - mu), axis=-1, keepdims=True)
        y = (y - mu) * jax.lax.rsqrt(var + LN_EPS) * ln_gamma + ln_beta
        out = jnp.einsum('bhwd,od->bhwo', y, out_proj_w)
        return out

    def _gn(v, G=32, eps=1e-5):
        B_, H_, W_, C_ = v.shape
        g = v.reshape(B_, H_, W_, G, C_ // G)
        m = jnp.mean(g, axis=(1, 2, 4), keepdims=True)
        s = jnp.var(g, axis=(1, 2, 4), keepdims=True)
        return ((g - m) / jnp.sqrt(s + eps)).reshape(v.shape)

    def _ln_c(v, eps=1e-6):
        m = jnp.mean(v, axis=-1, keepdims=True)
        s = jnp.var(v, axis=-1, keepdims=True)
        return (v - m) / jnp.sqrt(s + eps)

    def _ln_t(v, eps=1e-5):
        m = jnp.mean(v, axis=-1, keepdims=True)
        s = jnp.var(v, axis=-1, keepdims=True)
        return (v - m) / jnp.sqrt(s + eps)

    def _to_tokens(v):
        B_, H_, W_, C_ = v.shape
        return v.reshape(B_, H_ * W_, C_)
    def _from_tokens(t, like):
        return t.reshape(like.shape)

    x = x + _L0_conv_ref(_gn(x), L0_conv_in_proj_weight, L0_conv_out_proj_weight, L0_conv_x_proj_weight, L0_conv_dt_projs_weight, L0_conv_dt_projs_bias, L0_conv_A_logs, L0_conv_Ds, L0_conv_out_norm_weight, L0_conv_out_norm_bias)
    x = x + _L1_conv_ref(_gn(x), L1_conv_in_proj_w, L1_conv_conv_w, L1_conv_conv_b, L1_conv_x_proj_w, L1_conv_dt_w, L1_conv_dt_bias, L1_conv_A_logs, L1_conv_Ds, L1_conv_ln_w, L1_conv_ln_b, L1_conv_out_proj_w)
    x = x + _L2_conv_ref(_gn(x), L2_conv_in_proj_w, L2_conv_conv_w, L2_conv_conv_b, L2_conv_x_proj_weight, L2_conv_dt_projs_weight, L2_conv_dt_projs_bias, L2_conv_A_logs, L2_conv_Ds, L2_conv_ln_gamma, L2_conv_ln_beta, L2_conv_out_proj_w)
    x = x + _L3_conv_ref(_gn(x), L3_conv_in_proj_w, L3_conv_conv_w, L3_conv_conv_b, L3_conv_x_proj_weight, L3_conv_dt_projs_weight, L3_conv_dt_projs_bias, L3_conv_A_logs, L3_conv_Ds, L3_conv_ln_gamma, L3_conv_ln_beta, L3_conv_out_proj_w)
    return x


_drawn_inputs = setup_inputs


def setup_inputs(seed=0):
    import zlib

    import numpy as np

    out = dict(_drawn_inputs(seed))
    spreads = {'L0_conv_Ds': (1.0, 0.6),
     'L0_conv_out_norm_weight': (1.0, 0.2),
     'L0_conv_out_norm_bias': (0.0, 0.1),
     'L1_conv_conv_b': (0.0, 0.1),
     'L1_conv_Ds': (1.0, 0.6),
     'L1_conv_ln_w': (1.0, 0.6),
     'L1_conv_ln_b': (0.0, 0.8),
     'L2_conv_conv_b': (0.0, 0.1),
     'L2_conv_Ds': (1.0, 0.6),
     'L2_conv_ln_gamma': (1.0, 0.2),
     'L2_conv_ln_beta': (0.0, 0.1),
     'L3_conv_conv_b': (0.0, 0.1),
     'L3_conv_Ds': (1.0, 0.6),
     'L3_conv_ln_gamma': (1.0, 0.2),
     'L3_conv_ln_beta': (0.0, 0.289)}
    factors = {'L0_conv_x_proj_weight': 4.457,
     'L0_conv_dt_projs_weight': 8.0,
     'L0_conv_dt_projs_bias': 6.762,
     'L0_conv_A_logs': 8.0,
     'L1_conv_conv_w': 5.72,
     'L1_conv_x_proj_w': 64.0,
     'L1_conv_dt_w': 64.0,
     'L1_conv_dt_bias': 64.0,
     'L1_conv_A_logs': 64.0,
     'L2_conv_x_proj_weight': 2.716,
     'L2_conv_dt_projs_weight': 7.568,
     'L2_conv_dt_projs_bias': 3.876,
     'L2_conv_A_logs': 7.124}
    for name, (base, spread) in spreads.items():
        noise = np.random.default_rng([zlib.crc32(name.encode()), seed]).standard_normal(out[name].shape)
        drawn = base * np.exp(spread * noise) if base else spread * noise
        out[name] = jnp.asarray(drawn.astype(out[name].dtype))
    for name, factor in factors.items():
        out[name] = (out[name] * factor).astype(out[name].dtype)
    return out
```

```python
import numpy as np
import concourse.bass as bass
from concourse import mybir
from contextlib import ExitStack

F32 = mybir.dt.float32
ALU = mybir.AluOpType
ACT = mybir.ActivationFunctionType
AX = mybir.AxisListType

P = 128
IMAGES, H, W = 4, 64, 64
L = H * W
DM, DI, NS, K = 192, 384, 16, 4
GROUPS = 32
CB = 96
NCB = DM // CB
NDB = DI // P
T = 512
NCH = L // T
RW = T // W
SG = 4
NG = NS // SG
ITEMS = NG * NDB
RING = 4
PW = W + 2
TAPS = 9
PE_TAPS = 4
GN_EPS = 1e-5
LN_EPS = (1e-6, 1e-6, 1e-5, 1e-5)
RANK = (12, 12, 96)
MAX_LOG = 83.0
LN_SLACK = 2.0 ** -23

V_DTB = 0
V_D = V_DTB + K * NDB
V_ALOG = V_D + K * NDB
V_LNW = V_ALOG + K * NDB * NS
V_LNB = V_LNW + NDB
V_CB = V_LNB + NDB
V_TAP = V_CB + NDB
V_ALL = V_TAP + NDB * TAPS

LAYERS = 4


def wait(eng, sem, value):
    if not (isinstance(value, int) and value <= 0):
        eng.wait_ge(sem, value)


def build(nc, x_in, ident_in, group_in, ones_in, w_in, w_out, w_xp, w_dt, vecs, out):
    ctx = ExitStack()
    with ctx:
        def sb(name, shape):
            return ctx.enter_context(nc.sbuf_tensor(name, shape, F32))

        ident = sb("ident", [P, P])
        group_mean = sb("group_mean", [CB, CB])
        chan_mean = sb("chan_mean", [P, P])
        vec = sb("vec", [P, V_ALL])
        a_neg = sb("a_neg", [P, K, NDB, NS])
        dsum = sb("dsum", [P, NDB])
        gn_mean = sb("gn_mean", [CB, NCB])
        gn_sum = sb("gn_sum", [CB, NCB])
        gn_rstd = sb("gn_rstd", [CB, NCB])
        gn_bias = sb("gn_bias", [CB, NCB])
        ln_eps = sb("ln_eps", [P, 1])
        gn_eps = sb("gn_eps", [CB, 1])
        xp_w = sb("xp_w", [P, K, NDB, P])
        dt_w = sb("dt_w", [CB, K, DI])
        u = sb("u", [P, NDB, L])
        pad = sb("pad", [P, NDB, PW * PW])
        y_acc = pad[:, :, 0:L]
        regA = sb("regA", [P, 2 * 2 * SG * T + RING * SG * T])
        regB = sb("regB", [P, 2 * 2 * NDB * T + 2 * T + 2 * 3 * T + T])

        xT = regA[0:CB, 0:NCB * L].rearrange("p (c t) -> p c t", c=NCB)
        spare = regA[:, NCB * L:2 * NCB * L]
        bc = regA[:, 0:4 * SG * T].rearrange("p (q b n t) -> p q b n t", q=2, b=2, n=SG)
        ring = regA[:, 4 * SG * T:].rearrange("p (r n t) -> p r n t", r=RING, n=SG)
        o = 0
        dt = regB[:, o:o + 2 * NDB * T].rearrange("p (q d t) -> p q d t", q=2, d=NDB); o += 2 * NDB * T
        dtu = regB[:, o:o + 2 * NDB * T].rearrange("p (q d t) -> p q d t", q=2, d=NDB); o += 2 * NDB * T
        dts = regB[:, o:o + 2 * T].rearrange("p (q t) -> p q t", q=2); o += 2 * T
        sp_t = regB[:, o:o + 6 * T].rearrange("p (q s t) -> p q s t", q=2, s=3); o += 6 * T
        xd_sb = regB[:, o:o + T]
        xd_sb2 = regB[:, 0:2 * T].rearrange("p (q t) -> p q t", q=2)
        carry = sb("carry", [P, NDB, NS])

        o = 0
        in_w = regB[0:CB, o:o + NCB * 2 * DI].rearrange("p (c e) -> p c e", c=NCB); o += NCB * 2 * DI
        out_w = regB[:, o:o + NDB * DM].rearrange("p (d c) -> p d c", d=NDB); o += NDB * DM
        tap_w = regB[:, o:o + PE_TAPS * NDB * P].rearrange("p (k d j) -> p k d j", k=PE_TAPS, d=NDB)
        gn_junk = spare[0:CB, 0:L]
        xn = spare[0:CB, 0:2 * NCB * T].rearrange("p (q c t) -> p q c t", q=2, c=NCB)
        cv = spare[:, 2 * NCB * T:(2 * NCB + 2 * NDB) * T].rearrange("p (q d t) -> p q d t", q=2, d=NDB)
        yc = spare[:, 0:2 * NDB * T].rearrange("p (q d t) -> p q d t", q=2, d=NDB)
        rs = spare[:, 2 * NDB * T:(2 * NDB + 2) * T].rearrange("p (q t) -> p q t", q=2)
        sq = regB[:, o:o + 2 * NDB * T].rearrange("p (q d t) -> p q d t", q=2, d=NDB)

        ps = ctx.enter_context(nc.psum_tensor("ps", [P, 8, T], F32))

        xd_dram = [nc.dram_tensor(f"xd_{l}", (K, NCH, RANK[l] + 2 * NS, T), F32).ap() for l in range(3)]
        x_dram = nc.dram_tensor("x_keep", (CB, NCB, L), F32).ap()

        sems = [ctx.enter_context(nc.semaphore(f"s{i}")) for i in range(32)]
        all_sems = range(sems[0].num, sems[-1].num + 1)
        assert [s.num for s in sems] == list(all_sems)

        def image_of(ap, b):
            return ap[bass.ds(b, 1)].rearrange("o p c t -> (o p) c t")

        def in_order(view, k, d, n):
            at = n if k < 2 else n * -1 + (NCH - 1)
            v = view[:, d, :]
            if k % 2 == 0:
                return v[:, bass.ds(at * T, T)]
            return v.rearrange("p (h w) -> p w h", w=W)[:, bass.ds(at * RW, RW), :]

        def as_chunk(tile, k):
            return tile if k % 2 == 0 else tile.rearrange("p (w h) -> p w h", h=H)

        with nc.Block(no_gpsimd_drain=True) as block:
            loaded, = sems[:1]

            @block.sync
            def _(sp):
                sp.dma_start(ident[:], ident_in).then_inc(loaded, 16)
                sp.dma_start(group_mean[:], group_in).then_inc(loaded, 16)
                sp.dma_start(chan_mean[:], ones_in).then_inc(loaded, 16)
                sp.wait_ge(loaded, 48)

            @block.vector
            def _(dve):
                nc.vector.memset(gn_eps[:], GN_EPS)
        nc.all_engine_barrier(sems_to_clear=all_sems)

        def norm_conv(l, b):
            conv, last = l > 0, l == 3
            (x_ready, w_ready, x_saved, sum_made, sum_mm, mean_made, sq_made, var_mm, rstd_made,
             bias_made, tap_made, border, xn_made, in_mm, pad_made, cv_mm, cv_step,
             cv_used, act_own, dve_own, a_made) = sems[:21]
            weights = 48 if last else 80
            XN_FREE, PAD_FREE = 2, 2
            CV_FREE = 2 * NDB
            DT_TAPS = TAPS - PE_TAPS
            STEP_FREE = CV_FREE * DT_TAPS

            with nc.Block(no_gpsimd_drain=True) as block:
                @block.sync
                def _(sp):
                    if l == 0:
                        sp.dma_start(xT, image_of(x_in, b)).then_inc(x_ready, 16)
                    sp.dma_start(vec[:], vecs[l]).then_inc(w_ready, 16)
                    sp.dma_start(in_w, w_in[l]).then_inc(w_ready, 16)
                    sp.dma_start(out_w, w_out[l]).then_inc(w_ready, 16)
                    if not last:
                        M = RANK[l] + 2 * NS
                        sp.dma_start(xp_w[:, :, :, 0:M], w_xp[l]).then_inc(w_ready, 16)
                        sp.dma_start(dt_w[0:RANK[l]], w_dt[l]).then_inc(w_ready, 16)
                    if l in (1, 2):
                        sp.dma_start(x_dram, xT).then_inc(x_saved, 16)
                        sp.wait_ge(x_saved, 16)
                    if l == 0:
                        sp.wait_ge(x_ready, 16)
                    sp.wait_ge(w_ready, weights)

                @block.gpsimd
                def _(pool):
                    if conv:
                        v = pad[:].rearrange("p d (h w) -> p d h w", w=PW)
                        nc.gpsimd.memset(v[:, :, 0, :], 0.0).then_inc(border, 1)
                        nc.gpsimd.memset(v[:, :, PW - 1, :], 0.0).then_inc(border, 1)
                        nc.gpsimd.memset(v[:, :, 1:PW - 1, 0], 0.0).then_inc(border, 1)
                        nc.gpsimd.memset(v[:, :, 1:PW - 1, PW - 1], 0.0).then_inc(border, 1)

                @block.vector
                def _(dve):
                    dve.sem_inc(pad_made, PAD_FREE)
                    if conv:
                        dve.sem_inc(cv_step, STEP_FREE)
                    if l == 0:
                        dve.wait_ge(x_ready, 16)
                    nc.vector.tensor_reduce(gn_sum[:], xT, AX.X, ALU.add).then_inc(sum_made, 1)
                    dve.wait_ge(sum_mm, 1)
                    nc.vector.tensor_scalar(gn_mean[:], ps[0:CB, 6, 0:NCB], -1.0, None,
                                            ALU.mult).then_inc(mean_made, 1)
                    dve.wait_ge(w_ready, weights)
                    nc.vector.memset(ln_eps[:], LN_EPS[l]).then_inc(dve_own, 1)
                    dv = vec[:, V_D:V_D + K * NDB].rearrange("p (k d) -> p d k", k=K)
                    nc.vector.tensor_reduce(dsum[:], dv, AX.X, ALU.add).then_inc(dve_own, 1)
                    if last:
                        dve.wait_ge(dve_own, 2)
                        nc.vector.tensor_scalar(dsum[:], dsum[:], 1.0 / K, None, ALU.mult)
                    else:
                        al = vec[:, V_ALOG:V_ALOG + K * NDB * NS]
                        av = a_neg[:].rearrange("p k d n -> p (k d n)")
                        nc.vector.tensor_scalar(av, al, MAX_LOG, None, ALU.min).then_inc(dve_own, 1)
                        dve.wait_ge(a_made, 1)
                        nc.vector.tensor_scalar(av, av, -1.0, None, ALU.mult)
                    dve.wait_ge(rstd_made, 1)
                    nc.vector.tensor_tensor(gn_bias[:], gn_mean[:], gn_rstd[:],
                                            ALU.mult).then_inc(bias_made, 1)
                    v = pad[:].rearrange("p d (h w) -> p d h w", w=PW)
                    if conv:
                        dve.wait_ge(border, 4)
                    with dve.Fori(0, NCH // 2) as j:
                        for q in range(2):
                            c = j * 2 + q
                            dve.wait_ge(in_mm, XN_FREE + c + 1)
                            src = ps[:, 3 * q:3 * q + NDB, :]
                            if conv:
                                src = src.rearrange("p d (r w) -> p d r w", w=W)
                                dst = v[:, :, bass.ds(c * RW + 1, RW), 1:1 + W]
                            else:
                                dst = u[:, :, bass.ds(c * T, T)]
                            nc.vector.tensor_copy(dst, src).then_inc(pad_made, 1)
                    if not conv:
                        return
                    dve.wait_ge(pad_made, PAD_FREE + NCH)
                    with dve.Fori(0, NCH // 2) as j:
                        for q in range(2):
                            c = j * 2 + q
                            for s in range(DT_TAPS):
                                tap = PE_TAPS + s
                                for d in range(NDB):
                                    dst = cv[:, q, d, :].rearrange("p (r w) -> p r w", w=W)
                                    src = v[:, d, bass.ds(c * RW + tap // 3, RW),
                                            tap % 3:tap % 3 + W]
                                    wt = vec[:, V_TAP + d * TAPS + tap:V_TAP + d * TAPS + tap + 1]
                                    if s == 0:
                                        dve.wait_ge(cv_mm, c * NDB + d + 1)
                                        dve.wait_ge(cv_used, c * NDB + d + 1)
                                        part = ps[:, 3 * q + d, :].rearrange("p (r w) -> p r w", w=W)
                                    else:
                                        dve.wait_ge(cv_step, STEP_FREE + c * NDB * DT_TAPS
                                                    + NDB * (s - 1) + d + 1)
                                        part = dst
                                    nc.vector.scalar_tensor_tensor(
                                        dst, src, wt, part, ALU.mult, ALU.add).then_inc(cv_step, 1)

                @block.scalar
                def _(act):
                    if conv:
                        act.sem_inc(cv_used, CV_FREE)
                    nc.scalar.preload_act_table_set("natural_log_exp_and_others")
                    act.wait_ge(mean_made, 1)
                    for c in range(NCB):
                        if c:
                            act.wait_ge(sq_made, c)
                        nc.scalar.activation(gn_junk, xT[:, c, :], ACT.Square,
                                             bias=gn_mean[:, c:c + 1],
                                             accum_out=gn_sum[:, c:c + 1]).then_inc(sq_made, 1)
                    if not last:
                        act.wait_ge(dve_own, 3)
                        av = a_neg[:].rearrange("p k d n -> p (k d n)")
                        nc.scalar.activation(av, av, ACT.Exp).then_inc(a_made, 1)
                    act.wait_ge(var_mm, 1)
                    nc.scalar.activation(gn_rstd[:], ps[0:CB, 6, 0:NCB], ACT.Ln,
                                         bias=gn_eps[:]).then_inc(act_own, 1)
                    act.wait_ge(act_own, 1)
                    nc.scalar.activation(gn_rstd[:], gn_rstd[:], ACT.Exp,
                                         scale=-0.5).then_inc(rstd_made, 1)
                    if conv:
                        nc.scalar.preload_act_table_set("silu_and_others")
                    act.wait_ge(bias_made, 1)
                    with act.Fori(0, NCH // 2) as j:
                        for q in range(2):
                            c = j * 2 + q
                            act.wait_ge(in_mm, c + 1)
                            for cb in range(NCB):
                                nc.scalar.activation(xn[:, q, cb, :], xT[:, cb, bass.ds(c * T, T)],
                                                     ACT.Identity, bias=gn_bias[:, cb:cb + 1],
                                                     scale=gn_rstd[:, cb:cb + 1]).then_inc(xn_made, 1)
                    if not conv:
                        return
                    act.wait_ge(w_ready, weights)
                    for tap in range(PE_TAPS):
                        for d in range(NDB):
                            j = V_TAP + d * TAPS + tap
                            nc.scalar.activation(tap_w[:, tap, d, :], ident[:], ACT.Copy,
                                                 scale=vec[:, j:j + 1]).then_inc(tap_made, 1)
                    with act.Fori(0, NCH // 2) as j:
                        for q in range(2):
                            c = j * 2 + q
                            for d in range(NDB):
                                act.wait_ge(cv_step, STEP_FREE + c * NDB * DT_TAPS
                                            + NDB * (DT_TAPS - 1) + d + 1)
                                nc.scalar.activation(u[:, d, bass.ds(c * T, T)], cv[:, q, d, :],
                                                     ACT.Silu, bias=vec[:, V_CB + d:V_CB + d + 1]
                                                     ).then_inc(cv_used, 1)

                @block.tensor
                def _(pe):
                    pe.sem_inc(in_mm, XN_FREE)
                    pe.wait_ge(sum_made, 1)
                    nc.tensor.matmul(ps[0:CB, 6, 0:NCB], group_mean[:], gn_sum[:],
                                     start=True, stop=True).then_inc(sum_mm, 1)
                    pe.wait_ge(sq_made, NCB)
                    nc.tensor.matmul(ps[0:CB, 6, 0:NCB], group_mean[:], gn_sum[:],
                                     start=True, stop=True).then_inc(var_mm, 1)
                    pe.wait_ge(w_ready, weights)
                    with pe.Fori(0, NCH // 2) as j:
                        for q in range(2):
                            c = j * 2 + q
                            pe.wait_ge(xn_made, c * NCB + NCB)
                            pe.wait_ge(pad_made, c + 1)
                            for d in range(NDB):
                                for cb in range(NCB):
                                    last_mm = nc.tensor.matmul(
                                        ps[:, 3 * q + d, :], in_w[:, cb, d * P:(d + 1) * P],
                                        xn[:, q, cb, :], start=cb == 0, stop=cb == NCB - 1)
                            last_mm.then_inc(in_mm, 1)
                    if not conv:
                        return
                    v = pad[:].rearrange("p d (h w) -> p d h w", w=PW)
                    pe.wait_ge(tap_made, PE_TAPS * NDB)
                    pe.wait_ge(border, 4)
                    pe.wait_ge(pad_made, PAD_FREE + NCH)
                    with pe.Fori(0, NCH // 2) as j:
                        for q in range(2):
                            c = j * 2 + q
                            for d in range(NDB):
                                pe.wait_ge(cv_step, c * NDB * DT_TAPS + d + 1)
                                for tap in range(PE_TAPS):
                                    last_mm = nc.tensor.matmul(
                                        ps[:, 3 * q + d, :].rearrange("p (r w) -> p r w", w=W),
                                        tap_w[:, tap, d, :],
                                        v[:, d, bass.ds(c * RW + tap // 3, RW), tap % 3:tap % 3 + W],
                                        start=tap == 0, stop=tap == PE_TAPS - 1)
                                last_mm.then_inc(cv_mm, 1)
            nc.all_engine_barrier(sems_to_clear=all_sems)

        def scan(l):
            R = RANK[l]
            M = R + 2 * NS
            (bc_q0, bc_q1, dts_q0, dts_q1, xd_mm, xd_copied, xd_pre, xd_stored, z_mm, z_read,
             sp_abs, sp_exp, sp_ready, sp_half, dt_made, dtu_made, b_made, a_made, scanned,
             carried, g_made, y_mm, y_read) = sems[:23]
            bc_loaded, dts_loaded = (bc_q0, bc_q1), (dts_q0, dts_q1)
            Y_BANK, M_BANK = 4, 7
            PRE_FREE = 2
            COPIED = PRE_FREE + NCH
            PE_Z = (0, 2, 4)
            ACT_SP = (3, 5, 7)
            DVE_SP = (5, 7, 9)
            POOL_SP = (6, 8, 10)
            PE_XD, ACT_XD = 7, 10

            def chunk(k, n, half):
                return k, n, half, k * NCH + n

            def chunks(eng, step):
                for k in range(K):
                    before = chunk(k - 1, NCH - 1, NCH // 2 - 1) if k else None
                    after = chunk(k + 1, 0, 0) if k + 1 < K else None
                    step(chunk(k, 0, 0), before, chunk(k, 1, 0), 0)
                    with eng.Fori(0, NCH // 2 - 1) as j:
                        c = [chunk(k, j * 2 + i, j + i // 2) for i in range(4)]
                        step(c[1], c[0], c[2], 1)
                        step(c[2], c[1], c[3], 0)
                    step(chunk(k, NCH - 1, NCH // 2 - 1), chunk(k, NCH - 2, NCH // 2 - 1), after, 1)

            def xd_of(k, n):
                return xd_dram[l][k][bass.ds(n, 1)].rearrange("o m t -> (o m) t")

            with nc.Block(no_gpsimd_drain=True) as block:
                @block.sync
                def _(sp):
                    def load_dts(c, par):
                        k, n, _, S = c
                        wait(sp, z_mm, NDB * (S - 1))
                        sp.dma_start(dts[0:R, par, :], xd_of(k, n)[0:R]).then_inc(dts_loaded[par], 16)

                    sp.sem_inc(xd_pre, 16 * PRE_FREE)
                    for n in range(NCH):
                        sp.wait_ge(xd_copied, PRE_FREE + n + 1)
                        sp.wait_ge(xd_pre, (PRE_FREE + n) * 16)
                        sp.dma_start(xd_of(0, n), xd_sb2[0:M, n % 2, :]).then_inc(xd_pre, 16)
                    sp.wait_ge(xd_pre, (PRE_FREE + NCH) * 16)
                    load_dts(chunk(0, 0, 0), 0)

                    def step(this, before, after, par):
                        k, n, _, S = this
                        if after:
                            if after[0]:
                                sp.wait_ge(xd_stored, (after[3] - NCH + 1) * 16)
                            load_dts(after, 1 - par)
                        for g in range(NG):
                            wait(sp, b_made, (S * NG + g - 1) * NDB)
                            wait(sp, g_made, (S * NG + g - 1) * NDB)
                            src = xd_of(k, n)[R:M].rearrange("(b g n) t -> g b n t", b=2, g=NG)[g]
                            for b in range(2):
                                sp.dma_start(bc[:, g % 2, b], src[b].partition_broadcast(P)
                                             ).then_inc(bc_loaded[g % 2], 16)
                    chunks(sp, step)

                @block.tensor
                def _(pe):
                    def project_x(k, n, bank):
                        for d in range(NDB):
                            mm = nc.tensor.matmul(as_chunk(ps[0:M, bank, :], k),
                                                  xp_w[:, k, d, 0:M], in_order(u, k, d, n),
                                                  start=d == 0, stop=d == NDB - 1)
                        mm.then_inc(xd_mm, 1)

                    def project_dt(c, d, par):
                        k, n, half, S = c
                        wait(pe, z_read, S * NDB + d)
                        if d == 0:
                            pe.wait_ge(dts_loaded[par], (half + (k * NCH // 2 + 1)) * 16)
                        nc.tensor.matmul(ps[:, M_BANK, :], dt_w[0:R, k, d * P:(d + 1) * P],
                                         dts[0:R, par, :], start=True, stop=True).then_inc(z_mm, 1)

                    with pe.Fori(0, NCH // 2) as j:
                        for q in range(2):
                            n = j * 2 + q
                            pe.wait_ge(xd_copied, n + 1)
                            project_x(0, n, q)
                    for d in range(NDB):
                        project_dt(chunk(0, 0, 0), d, 0)

                    def step(this, before, after, par):
                        k, n, _, S = this
                        for i in range(ITEMS):
                            g, d = divmod(i, NDB)
                            if after and i in PE_Z:
                                if i == 0 and (k + 1 < K or isinstance(n, int) and n == 0):
                                    pe.wait_ge(xd_copied, S + COPIED)
                                project_dt(after, PE_Z.index(i), 1 - par)
                            if i == PE_XD and k + 1 < K:
                                pe.wait_ge(z_read, (S + 2) * NDB)
                                project_x(k + 1, n, M_BANK)
                            if g == 0:
                                wait(pe, y_read, (S - 1) * NDB + d + 1)
                            pe.wait_ge(g_made, S * ITEMS + i + 1)
                            for s in range(SG):
                                mm = nc.tensor.matmul(ps[:, Y_BANK + d, :], ident[:],
                                                      ring[:, i % RING, s, :],
                                                      start=g == 0 and s == 0,
                                                      stop=g == NG - 1 and s == SG - 1)
                            mm.then_inc(y_mm, 1)
                    chunks(pe, step)

                @block.scalar
                def _(act):
                    def softplus(c, d, part, par):
                        k, n, _, S = c
                        t = sp_t[:, (par + d) % 2]
                        bias = vec[:, V_DTB + k * NDB + d:V_DTB + k * NDB + d + 1]
                        z = S * NDB + d
                        if part == 0:
                            act.wait_ge(z_mm, z + 1)
                            wait(act, dt_made, z - 1)
                            nc.scalar.activation(t[:, 0, :], ps[:, M_BANK, :], ACT.Abs,
                                                 bias=bias).then_inc(sp_abs, 1)
                            nc.scalar.activation(t[:, 1, :], ps[:, M_BANK, :], ACT.Relu,
                                                 bias=bias).then_inc(z_read, 1)
                        elif part == 1:
                            act.wait_ge(sp_abs, z + 1)
                            nc.scalar.activation(t[:, 0, :], t[:, 0, :], ACT.Exp,
                                                 scale=-1.0).then_inc(sp_exp, 1)
                        else:
                            act.wait_ge(sp_exp, z + 1)
                            nc.scalar.activation(t[:, 2, :], t[:, 0, :], ACT.Ln,
                                                 bias=1.0).then_inc(sp_ready, 1)

                    nc.scalar.preload_act_table_set("natural_log_exp_and_others")
                    act.sem_inc(xd_copied, PRE_FREE)
                    with act.Fori(0, NCH // 2) as j:
                        for q in range(2):
                            n = j * 2 + q
                            act.wait_ge(xd_mm, n + 1)
                            act.wait_ge(xd_pre, (n + 1) * 16)
                            nc.scalar.activation(xd_sb2[0:M, q, :], ps[0:M, q, :],
                                                 ACT.Copy).then_inc(xd_copied, 1)
                    for d in range(NDB):
                        for part in range(3):
                            softplus(chunk(0, 0, 0), d, part, 0)

                    def step(this, before, after, par):
                        k, n, _, S = this
                        for i in range(ITEMS):
                            g, d = divmod(i, NDB)
                            if g == 0:
                                act.wait_ge(dt_made, S * NDB + d + 1)
                            for s in range(SG):
                                wait(act, scanned, (S * ITEMS + i - 1) * SG + s + 1)
                                nc.scalar.activation(
                                    ps[:, s, :], dt[:, par, d, :], ACT.Exp,
                                    scale=a_neg[:, k, d, g * SG + s:g * SG + s + 1]).then_inc(a_made, 1)
                            if after:
                                for dn, at in enumerate(ACT_SP):
                                    if i - at in range(3):
                                        softplus(after, dn, i - at, 1 - par)
                            if k + 1 < K and i == ACT_XD:
                                act.wait_ge(xd_mm, S + NCH + 1)
                                wait(act, xd_stored, S * 16)
                                nc.scalar.activation(xd_sb[0:M], ps[0:M, M_BANK, :],
                                                     ACT.Copy).then_inc(xd_copied, 1)
                            if k + 1 < K and i == ACT_XD + 1:
                                act.wait_ge(xd_copied, S + COPIED + 1)
                                act.dma_start(xd_of(k + 1, n), xd_sb[0:M]).then_inc(xd_stored, 16)
                    chunks(act, step)

                @block.vector
                def _(dve):
                    def guard(c, d, par):
                        t = sp_t[:, (par + d) % 2]
                        dve.wait_ge(sp_ready, c[3] * NDB + d + 1)
                        nc.vector.scalar_tensor_tensor(t[:, 2, :], t[:, 2, :], LN_SLACK, t[:, 0, :],
                                                       ALU.add, ALU.min).then_inc(sp_half, 1)

                    def make_dt(c, d, par):
                        t = sp_t[:, (par + d) % 2]
                        dve.wait_ge(sp_half, c[3] * NDB + d + 1)
                        nc.vector.tensor_tensor(dt[:, par, d, :], t[:, 2, :], t[:, 1, :],
                                                ALU.add).then_inc(dt_made, 1)

                    def make_input(c, i, par):
                        g, d = divmod(i, NDB)
                        S = c[3]
                        if g == 0:
                            dve.wait_ge(dtu_made, S * NDB + d + 1)
                        if d == 0:
                            dve.wait_ge(bc_loaded[g % 2], (S * 2 + g // 2 + 1) * 32)
                        wait(dve, y_mm, S * ITEMS + i - RING + 1)
                        nc.vector.tensor_tensor(
                            ring[:, i % RING], dtu[:, par, d:d + 1, :].to_broadcast([P, SG, T]),
                            bc[:, g % 2, 0], ALU.mult).then_inc(b_made, 1)

                    def add_y(c, d):
                        k, n, _, S = c
                        dve.wait_ge(y_mm, S * ITEMS + ITEMS - NDB + d + 1)
                        y = in_order(y_acc, k, d, n)
                        part = as_chunk(ps[:, Y_BANK + d, :], k)
                        if k == 0:
                            nc.vector.scalar_tensor_tensor(y, in_order(u, k, d, n), dsum[:, d:d + 1],
                                                           part, ALU.mult, ALU.add).then_inc(y_read, 1)
                        else:
                            nc.vector.tensor_tensor(y, y, part, ALU.add).then_inc(y_read, 1)

                    for d in range(NDB):
                        guard(chunk(0, 0, 0), d, 0)
                        make_dt(chunk(0, 0, 0), d, 0)
                    make_input(chunk(0, 0, 0), 0, 0)

                    def step(this, before, after, par):
                        k, n, _, S = this
                        for i in range(ITEMS):
                            g, d = divmod(i, NDB)
                            dve.wait_ge(b_made, S * ITEMS + i + 1)
                            for s in range(SG):
                                dve.wait_ge(a_made, (S * ITEMS + i) * SG + s + 1)
                                h = ring[:, i % RING, s, :]
                                st = g * SG + s
                                first = isinstance(n, int) and n == 0
                                decay = ps[:, s, :]
                                if k >= 2:
                                    h, decay = h[:, ::-1], decay[:, ::-1]
                                nc.vector.tensor_tensor_scan(
                                    h, decay, h, 0.0 if first else carry[:, d, st:st + 1],
                                    ALU.mult, ALU.add).then_inc(scanned, 1)
                            if i + 1 < ITEMS:
                                make_input(this, i + 1, par)
                            elif after:
                                make_input(after, 0, 1 - par)
                            dve.wait_ge(scanned, (S * ITEMS + i + 1) * SG)
                            nc.vector.tensor_copy(carry[:, d, g * SG:(g + 1) * SG],
                                                  ring[:, i % RING, :, T - 1 if k < 2 else 0]).then_inc(carried, 1)
                            if before and i < NDB:
                                add_y(before, i)
                            if after:
                                for dn, at in enumerate(DVE_SP):
                                    if i == at:
                                        guard(after, dn, 1 - par)
                                    if i == at + 1:
                                        make_dt(after, dn, 1 - par)
                    chunks(dve, step)
                    for d in range(NDB):
                        add_y(chunk(K - 1, NCH - 1, NCH // 2 - 1), d)

                @block.gpsimd
                def _(pool):
                    def make_dtu(c, d, par):
                        k, n, _, S = c
                        pool.wait_ge(dt_made, S * NDB + d + 1)
                        nc.gpsimd.tensor_tensor(as_chunk(dtu[:, par, d, :], k),
                                                as_chunk(dt[:, par, d, :], k),
                                                in_order(u, k, d, n), ALU.mult).then_inc(dtu_made, 1)

                    for d in range(NDB):
                        make_dtu(chunk(0, 0, 0), d, 0)

                    def step(this, before, after, par):
                        S = this[3]
                        for i in range(ITEMS):
                            g, d = divmod(i, NDB)
                            if d == 0:
                                pool.wait_ge(bc_loaded[g % 2], (S * 2 + g // 2 + 1) * 32)
                            pool.wait_ge(carried, S * ITEMS + i + 1)
                            nc.gpsimd.tensor_tensor(ring[:, i % RING], ring[:, i % RING],
                                                    bc[:, g % 2, 1], ALU.mult).then_inc(g_made, 1)
                            if after and i in POOL_SP:
                                make_dtu(after, POOL_SP.index(i), 1 - par)
                    chunks(pool, step)
            nc.all_engine_barrier(sems_to_clear=all_sems)

        def out_proj(l, b):
            last = l == 3
            (x_ready, x_out, xn_made, in_mm, z_made, y_made, mean_mm, yc_made, sq_made, var_mm,
             ln_made, rs_made, yn_made, aff_made, gate_made, out_mm, res_made) = sems[:17]
            XN_FREE, Z_FREE = 2, 2
            ABASE = 0

            with nc.Block(no_gpsimd_drain=True) as block:
                @block.sync
                def _(sp):
                    if not last:
                        sp.dma_start(in_w, w_in[l]).then_inc(x_ready, 16)
                        sp.dma_start(out_w, w_out[l]).then_inc(x_ready, 16)
                        sp.dma_start(xT, image_of(x_in, b) if l == 0 else x_dram).then_inc(x_ready, 16)
                        sp.wait_ge(x_ready, 48)
                    else:
                        sp.wait_ge(res_made, NCH)
                        sp.dma_start(image_of(out, b), xT).then_inc(x_out, 16)
                        sp.wait_ge(x_out, 16)

                @block.tensor
                def _(pe):
                    pe.sem_inc(in_mm, XN_FREE)
                    if not last:
                        pe.wait_ge(x_ready, 48)
                    with pe.Fori(0, NCH // 2) as j:
                        for q in range(2):
                            c = j * 2 + q
                            pe.wait_ge(xn_made, c * NCB + NCB)
                            pe.wait_ge(z_made, c + 1)
                            for d in range(NDB):
                                for cb in range(NCB):
                                    mm = nc.tensor.matmul(
                                        ps[:, 3 * q + d, :], in_w[:, cb, DI + d * P:DI + (d + 1) * P],
                                        xn[:, q, cb, :], start=cb == 0, stop=cb == NCB - 1)
                            mm.then_inc(in_mm, 1)
                    pe.wait_ge(z_made, Z_FREE + NCH)
                    if last:
                        pe.wait_ge(y_made, NCH * NDB)
                    with pe.Fori(0, NCH // 2) as j:
                        for q in range(2):
                            c = j * 2 + q
                            for d in range(NDB):
                                mm = nc.tensor.matmul(ps[:, q, :], chan_mean[:],
                                                      y_acc[:, d, bass.ds(c * T, T)],
                                                      start=d == 0, stop=d == NDB - 1)
                            mm.then_inc(mean_mm, 1)
                        for q in range(2):
                            c = j * 2 + q
                            pe.wait_ge(sq_made, c + 1)
                            for d in range(NDB):
                                mm = nc.tensor.matmul(ps[:, 2 + q, :], chan_mean[:], sq[:, q, d, :],
                                                      start=d == 0, stop=d == NDB - 1)
                            mm.then_inc(var_mm, 1)
                        for q in range(2):
                            c = j * 2 + q
                            if last:
                                pe.wait_ge(aff_made, c * NDB + NDB)
                            else:
                                pe.wait_ge(gate_made, c + 1)
                            for cb in range(NCB):
                                for d in range(NDB):
                                    mm = nc.tensor.matmul(
                                        ps[0:CB, 4 + 2 * q + cb, :], out_w[:, d, cb * CB:(cb + 1) * CB],
                                        yc[:, q, d, :], start=d == 0, stop=d == NDB - 1)
                            mm.then_inc(out_mm, 1)

                @block.scalar
                def _(act):
                    act.sem_inc(z_made, Z_FREE)
                    if not last:
                        act.wait_ge(x_ready, 48)
                    nc.scalar.preload_act_table_set("silu_and_others")
                    with act.Fori(0, NCH // 2) as j:
                        for q in range(2):
                            c = j * 2 + q
                            act.wait_ge(in_mm, c + 1)
                            for cb in range(NCB):
                                nc.scalar.activation(xn[:, q, cb, :], xT[:, cb, bass.ds(c * T, T)],
                                                     ACT.Identity, bias=gn_bias[:, cb:cb + 1],
                                                     scale=gn_rstd[:, cb:cb + 1]).then_inc(xn_made, 1)
                        for q in range(2):
                            c = j * 2 + q
                            act.wait_ge(in_mm, XN_FREE + c + 1)
                            if last:
                                act.wait_ge(y_made, c * NDB)
                                dst = sq[:, q]
                            else:
                                dst = u[:, :, bass.ds(c * T, T)]
                            nc.scalar.activation(dst, ps[:, 3 * q:3 * q + NDB, :],
                                                 ACT.Silu).then_inc(z_made, 1)
                    nc.scalar.preload_act_table_set("natural_log_exp_and_others")
                    with act.Fori(0, NCH // 2) as j:
                        for q in range(2):
                            c = j * 2 + q
                            act.wait_ge(yc_made, c + 1)
                            nc.scalar.activation(sq[:, q], yc[:, q], ACT.Square).then_inc(sq_made, 1)
                        for q in range(2):
                            c = j * 2 + q
                            act.wait_ge(var_mm, c + 1)
                            nc.scalar.activation(rs[:, q, :], ps[:, 2 + q, :], ACT.Ln,
                                                 bias=ln_eps[:]).then_inc(ln_made, 1)
                            act.wait_ge(ln_made, c + 1)
                            nc.scalar.activation(rs[:, q, :], rs[:, q, :], ACT.Exp,
                                                 scale=-0.5).then_inc(rs_made, 1)
                        for q in range(2):
                            c = j * 2 + q
                            act.wait_ge(yn_made, c + 1)
                            for d in range(NDB):
                                nc.scalar.activation(yc[:, q, d, :], yc[:, q, d, :], ACT.Identity,
                                                     bias=vec[:, V_LNB + d:V_LNB + d + 1],
                                                     scale=vec[:, V_LNW + d:V_LNW + d + 1]
                                                     ).then_inc(aff_made, 1)

                @block.vector
                def _(dve):
                    if last:
                        with dve.Fori(0, NCH // 2) as j:
                            for q in range(2):
                                c = j * 2 + q
                                dve.wait_ge(z_made, Z_FREE + c + 1)
                                for d in range(NDB):
                                    nc.vector.scalar_tensor_tensor(
                                        y_acc[:, d, bass.ds(c * T, T)], u[:, d, bass.ds(c * T, T)],
                                        dsum[:, d:d + 1], sq[:, q, d, :], ALU.mult,
                                        ALU.mult).then_inc(y_made, 1)
                    with dve.Fori(0, NCH // 2) as j:
                        for q in range(2):
                            c = j * 2 + q
                            dve.wait_ge(mean_mm, c + 1)
                            nc.vector.tensor_tensor(
                                yc[:, q], y_acc[:, :, bass.ds(c * T, T)],
                                ps[:, q:q + 1, :].to_broadcast([P, NDB, T]),
                                ALU.subtract).then_inc(yc_made, 1)
                        for q in range(2):
                            c = j * 2 + q
                            dve.wait_ge(rs_made, c + 1)
                            nc.vector.tensor_tensor(
                                yc[:, q], yc[:, q], rs[:, q:q + 1, :].to_broadcast([P, NDB, T]),
                                ALU.mult).then_inc(yn_made, 1)
                        for q in range(2):
                            c = j * 2 + q
                            dve.wait_ge(out_mm, c + 1)
                            xc = xT[:, :, bass.ds(c * T, T)]
                            nc.vector.tensor_tensor(xc, xc, ps[0:CB, 4 + 2 * q:6 + 2 * q, :],
                                                    ALU.add).then_inc(res_made, 1)

                @block.gpsimd
                def _(pool):
                    if last:
                        return
                    pool.wait_ge(z_made, Z_FREE + NCH)
                    with pool.Fori(0, NCH // 2) as j:
                        for q in range(2):
                            c = j * 2 + q
                            pool.wait_ge(aff_made, c * NDB + NDB)
                            nc.gpsimd.tensor_tensor(yc[:, q], yc[:, q], u[:, :, bass.ds(c * T, T)],
                                                    ALU.mult).then_inc(gate_made, 1)
            nc.all_engine_barrier(sems_to_clear=all_sems)

        with nc.Fori(0, IMAGES) as b:
            for l in range(LAYERS):
                norm_conv(l, b)
                if l < 3:
                    scan(l)
                out_proj(l, b)
            if LAYERS < 4:
                with nc.Block(no_gpsimd_drain=True) as block:
                    @block.sync
                    def _(sp):
                        sp.dma_start(image_of(out, b), xT).then_inc(sems[0], 16)
                        sp.wait_ge(sems[0], 16)
                nc.all_engine_barrier(sems_to_clear=all_sems)


def _blocks(a, blocks, axis):
    s = a.shape
    a = a.reshape(s[:axis] + (blocks, s[axis] // blocks) + s[axis + 1:])
    return np.ascontiguousarray(np.moveaxis(a, axis + 1, 0))


def kernel(**inputs):
    import concourse.bacc as bacc
    from concourse.bass_utils import run_bass_kernel_spmd

    a = {name: np.asarray(value) for name, value in inputs.items()}
    names = (
        dict(i="in_proj_weight", o="out_proj_weight", x="x_proj_weight", t="dt_projs_weight",
             tb="dt_projs_bias", w="out_norm_weight", b="out_norm_bias"),
        dict(i="in_proj_w", o="out_proj_w", x="x_proj_w", t="dt_w", tb="dt_bias", w="ln_w", b="ln_b"),
        dict(i="in_proj_w", o="out_proj_w", x="x_proj_weight", t="dt_projs_weight",
             tb="dt_projs_bias", w="ln_gamma", b="ln_beta"),
        dict(i="in_proj_w", o="out_proj_w", x="x_proj_weight", t="dt_projs_weight",
             tb="dt_projs_bias", w="ln_gamma", b="ln_beta"),
    )
    arrays = {
        "x": np.ascontiguousarray(
            a["x"].reshape(-1, L, NCB, CB).transpose(0, 3, 2, 1))[:IMAGES],
        "ident": np.eye(P, dtype=np.float32),
        "group_mean": np.kron(np.eye(CB * GROUPS // DM), np.full((DM // GROUPS,) * 2,
                              GROUPS / DM / L)).astype(np.float32),
        "chan_mean": np.full((P, P), 1.0 / DI, np.float32),
    }
    zeros = np.zeros
    for l, n in enumerate(names):
        def of(key):
            return a[f"L{l}_conv_{key}"]
        arrays[f"w_in{l}"] = _blocks(of(n["i"]).T, NCB, 0)
        arrays[f"w_out{l}"] = _blocks(of(n["o"]).T, NDB, 0)
        if l < 3:
            arrays[f"w_xp{l}"] = np.ascontiguousarray(
                _blocks(of(n["x"]), NDB, 2).transpose(0, 1, 3, 2))
            arrays[f"w_dt{l}"] = np.ascontiguousarray(of(n["t"]).transpose(2, 0, 1))
            skip = _blocks(of("Ds").reshape(K, DI), NDB, 1)
        else:
            skip = _blocks(of("Ds").reshape(DI, K).T, NDB, 1)
        if l == 0:
            taps, cb = zeros((P, NDB, TAPS), np.float32), zeros((P, NDB), np.float32)
        else:
            cw = of("conv_w").reshape(TAPS, DI).T if l == 3 else of("conv_w").reshape(DI, TAPS)
            taps, cb = _blocks(cw, NDB, 0), _blocks(of("conv_b"), NDB, 0)
        parts = (_blocks(of(n["tb"]), NDB, 1), skip, _blocks(of("A_logs").reshape(K, DI, NS), NDB, 1),
                 _blocks(of(n["w"]), NDB, 0), _blocks(of(n["b"]), NDB, 0), cb, taps)
        arrays[f"vec{l}"] = np.ascontiguousarray(
            np.concatenate([p.reshape(P, -1) for p in parts], axis=1))

    nc = bacc.Bacc("TRN2", target_bir_lowering=False, num_devices=1,
                   dynamic_dma_scratch_size=1024)
    ap = {name: nc.dram_tensor(name + "_in", v.shape, mybir.dt.from_np(v.dtype),
                               kind="ExternalInput").ap() for name, v in arrays.items()}
    out = nc.dram_tensor("x_out", (IMAGES, CB, NCB, L), F32, kind="ExternalOutput").ap()
    build(nc, ap["x"], ap["ident"], ap["group_mean"], ap["chan_mean"],
          [ap[f"w_in{l}"] for l in range(4)], [ap[f"w_out{l}"] for l in range(4)],
          [ap[f"w_xp{l}"] for l in range(3)], [ap[f"w_dt{l}"] for l in range(3)],
          [ap[f"vec{l}"] for l in range(4)], out)
    r = run_bass_kernel_spmd(nc, [{name + "_in": v for name, v in arrays.items()}], core_ids=[0])
    got = np.asarray(r.results[0]["x_out"])
    return np.ascontiguousarray(got.transpose(0, 3, 2, 1)).reshape(IMAGES, H, W, DM)
```

```python
import numpy as np
import concourse.bass as bass
from concourse import mybir
from contextlib import ExitStack

F32 = mybir.dt.float32
ALU = mybir.AluOpType
ACT = mybir.ActivationFunctionType
AX = mybir.AxisListType

P = 128
IMAGES, H, W = 4, 64, 64
L = H * W
DM, DI, NS, K = 192, 384, 16, 4
GROUPS = 32
CB = 96
NCB = DM // CB
NDB = DI // P
T = 512
NCH = L // T
RW = T // W
SG = 4
NG = NS // SG
ITEMS = NG * NDB
RING = 4
TP = T + 2
PW = W + 2
TAPS = 9
PE_TAPS = 4
GN_EPS = 1e-5
LN_EPS = (1e-6, 1e-6, 1e-5, 1e-5)
RANK = (12, 12, 96)
MAX_LOG = 83.0
LN_SLACK = 2.0 ** -23

V_DTB = 0
V_D = V_DTB + K * NDB
V_ALOG = V_D + K * NDB
V_LNW = V_ALOG + K * NDB * NS
V_LNB = V_LNW + NDB
V_CB = V_LNB + NDB
V_TAP = V_CB + NDB
V_ALL = V_TAP + NDB * TAPS


def wait(eng, sem, value):
    if not (isinstance(value, int) and value <= 0):
        eng.wait_ge(sem, value)


def build(nc, x_in, ident_in, group_in, ones_in, w_in, w_out, w_xp, w_dt, vecs, out):
    ctx = ExitStack()
    with ctx:
        def sb(name, shape):
            return ctx.enter_context(nc.sbuf_tensor(name, shape, F32))

        ident = sb("ident", [P, P])
        group_mean = sb("group_mean", [CB, CB])
        chan_mean = sb("chan_mean", [P, P])
        vec = sb("vec", [P, V_ALL])
        a_neg = sb("a_neg", [P, K, NDB, NS])
        dsum = sb("dsum", [P, NDB])
        gn_mean = sb("gn_mean", [CB, NCB])
        gn_chan = sb("gn_chan", [CB, NCB, 2])
        gn_dev = sb("gn_dev", [CB, NCB])
        gn_sum = sb("gn_sum", [CB, NCB])
        gn_rstd = sb("gn_rstd", [CB, NCB])
        gn_bias = sb("gn_bias", [CB, NCB])
        ln_eps = sb("ln_eps", [P, 1])
        gn_eps = sb("gn_eps", [CB, 1])
        xp_w = sb("xp_w", [P, 2, NDB, P])
        dt_w = sb("dt_w", [CB, 2, DI])
        u = sb("u", [P, NDB, L])
        pad = sb("pad", [P, NDB, PW * PW])
        y_acc = pad[:, :, 0:L]
        skip_w = pad[:, :, L:L + P]
        regA = sb("regA", [P, 2 * 2 * SG * T + RING * SG * TP])
        regB = sb("regB", [P, 2 * 2 * NDB * T + T + 2 * 2 * T + 2 * SG * TP])

        xT = regA[0:CB, 0:NCB * L].rearrange("p (c t) -> p c t", c=NCB)
        spare = regA[:, NCB * L:2 * NCB * L]
        bc = regA[:, 0:4 * SG * T].rearrange("p (q b n t) -> p q b n t", q=2, b=2, n=SG)
        ring = regA[:, 4 * SG * T:].rearrange("p (r n t) -> p r n t", r=RING, n=SG)
        runs = slice(1, 1 + T)
        o = 0
        dt = regB[:, o:o + 2 * NDB * T].rearrange("p (q d t) -> p q d t", q=2, d=NDB); o += 2 * NDB * T
        dtu = regB[:, o:o + 2 * NDB * T].rearrange("p (q d t) -> p q d t", q=2, d=NDB); o += 2 * NDB * T
        dts = regB[:, o:o + T]; o += T
        sp_t = regB[:, o:o + 4 * T].rearrange("p (q s t) -> p q s t", q=2, s=2); o += 4 * T
        decays = regB[:, o:o + 2 * SG * TP].rearrange("p (q s t) -> p q s t", q=2, s=SG)
        xd_sb2 = regB[:, 0:2 * T].rearrange("p (q t) -> p q t", q=2)
        carry = sb("carry", [P, NDB, NS])

        o = 0
        in_w = regB[0:CB, o:o + NCB * 2 * DI].rearrange("p (c e) -> p c e", c=NCB); o += NCB * 2 * DI
        out_w = regB[:, o:o + NDB * DM].rearrange("p (d c) -> p d c", d=NDB); o += NDB * DM
        tap_w = regB[:, o:o + PE_TAPS * NDB * P].rearrange("p (k d j) -> p k d j", k=PE_TAPS, d=NDB)
        xn = spare[0:CB, 0:2 * NCB * T].rearrange("p (q c t) -> p q c t", q=2, c=NCB)
        cv = spare[:, 2 * NCB * T:(2 * NCB + 2 * NDB) * T].rearrange("p (q d t) -> p q d t", q=2, d=NDB)
        yc = spare[:, 0:4 * NDB * T].rearrange("p (q d t) -> p q d t", q=4, d=NDB)
        rs = spare[:, 4 * NDB * T:(4 * NDB + 2) * T].rearrange("p (q t) -> p q t", q=2)
        y_sum = spare[:, (4 * NDB + 2) * T:(4 * NDB + 4) * T].rearrange("p (q t) -> p q t", q=2)
        sq = regB[:, o:o + 2 * NDB * T].rearrange("p (q d t) -> p q d t", q=2, d=NDB); o += 2 * NDB * T
        sq_sum = regB[:, o:o + 2 * T].rearrange("p (q t) -> p q t", q=2); o += 2 * T
        x_stats = regB[0:CB, o:o + NCB * NCH * 6].rearrange("p (c n s) -> p c n s", c=NCB, n=NCH)

        ps = ctx.enter_context(nc.psum_tensor("ps", [P, 8, T], F32))

        xd_dram = [nc.dram_tensor(f"xd_{l}", (K, NCH, RANK[l] + 2 * NS, T), F32).ap() for l in range(3)]
        x_dram = nc.dram_tensor("x_keep", (CB, NCB, L), F32).ap()

        sems = [ctx.enter_context(nc.semaphore(f"s{i}")) for i in range(32)]
        all_sems = range(sems[0].num, sems[-1].num + 1)
        assert [s.num for s in sems] == list(all_sems)

        def image_of(ap, b):
            return ap[bass.ds(b, 1)].rearrange("o p c t -> (o p) c t")

        def chunk_stats(c, sem):
            for cb in range(NCB):
                nc.vector.bn_stats(x_stats[:, cb, bass.ds(c, 1), :].rearrange("p o s -> p (o s)"),
                                   xT[:, cb, bass.ds(c * T, T)]).then_inc(sem, 1)

        def in_order(view, k, d, n):
            at = n if k < 2 else n * -1 + (NCH - 1)
            v = view[:, d, :]
            if k % 2 == 0:
                return v[:, bass.ds(at * T, T)]
            return v.rearrange("p (h w) -> p w h", w=W)[:, bass.ds(at * RW, RW), :]

        def as_chunk(tile, k):
            return tile if k % 2 == 0 else tile.rearrange("p (w h) -> p w h", h=H)

        with nc.Block(no_gpsimd_drain=True) as block:
            loaded, = sems[:1]

            @block.sync
            def _(sp):
                sp.dma_start(ident[:], ident_in).then_inc(loaded, 16)
                sp.dma_start(group_mean[:], group_in).then_inc(loaded, 16)
                sp.dma_start(chan_mean[:], ones_in).then_inc(loaded, 16)
                sp.wait_ge(loaded, 48)

            @block.vector
            def _(dve):
                nc.vector.memset(gn_eps[:], GN_EPS)
        nc.all_engine_barrier(sems_to_clear=all_sems)

        def norm_conv(l, b):
            conv, last = l > 0, l == 3
            (x_half0, x_half1, stats_made, in_loaded, w_ready, x_saved, sum_made, sum_mm, mean_made, sq_made, var_mm, rstd_made,
             bias_made, tap_made, border, xn_made, in_mm, pad_made, cv_mm, cv_step,
             cv_used, act_own, dve_own, a_made) = sems[:24]
            weights = 32 if last else 64
            XN_FREE, PAD_FREE = 2, 2
            CV_FREE = 2 * NDB
            DT_TAPS = TAPS - PE_TAPS
            STEP_FREE = CV_FREE * DT_TAPS

            with nc.Block(no_gpsimd_drain=True) as block:
                @block.sync
                def _(sp):
                    if l == 0:
                        for h, loaded in enumerate((x_half0, x_half1)):
                            at = slice(h * L // 2, (h + 1) * L // 2)
                            sp.dma_start(xT[:, :, at], image_of(x_in, b)[:, :, at]).then_inc(loaded, 16)
                    sp.dma_start(in_w, w_in[l]).then_inc(in_loaded, 16)
                    sp.dma_start(vec[:], vecs[l]).then_inc(w_ready, 16)
                    sp.dma_start(out_w, w_out[l]).then_inc(w_ready, 16)
                    if not last:
                        M = RANK[l] + 2 * NS
                        sp.dma_start(xp_w[:, :, :, 0:M], w_xp[l][:, 0:2]).then_inc(w_ready, 16)
                        sp.dma_start(dt_w[0:RANK[l]], w_dt[l][:, 0:2]).then_inc(w_ready, 16)
                    if l in (1, 2):
                        sp.dma_start(x_dram, xT).then_inc(x_saved, 16)
                        sp.wait_ge(x_saved, 16)
                    if l == 0:
                        sp.wait_ge(x_half0, 16)
                        sp.wait_ge(x_half1, 16)
                    sp.wait_ge(in_loaded, 16)
                    sp.wait_ge(w_ready, weights)

                @block.gpsimd
                def _(pool):
                    if conv:
                        v = pad[:].rearrange("p d (h w) -> p d h w", w=PW)
                        nc.gpsimd.memset(v[:, :, 0, :], 0.0).then_inc(border, 1)
                        nc.gpsimd.memset(v[:, :, PW - 1, :], 0.0).then_inc(border, 1)
                        nc.gpsimd.memset(v[:, :, 1:PW - 1, 0], 0.0).then_inc(border, 1)
                        nc.gpsimd.memset(v[:, :, 1:PW - 1, PW - 1], 0.0).then_inc(border, 1)

                @block.vector
                def _(dve):
                    dve.sem_inc(pad_made, PAD_FREE)
                    if conv:
                        dve.sem_inc(cv_step, STEP_FREE)
                    if l == 0:
                        for h, loaded in enumerate((x_half0, x_half1)):
                            dve.wait_ge(loaded, 16)
                            with dve.Fori(0, NCH // 2) as j:
                                chunk_stats(j + h * (NCH // 2), stats_made)
                        dve.wait_ge(stats_made, NCH * NCB)
                    for cb in range(NCB):
                        nc.vector.bn_aggr(gn_chan[:, cb, :],
                                          x_stats[:, cb].rearrange("p n s -> p (n s)")
                                          ).then_inc(sum_made, 1)
                    dve.wait_ge(sum_mm, 1)
                    nc.vector.tensor_scalar(gn_mean[:], ps[0:CB, 6, 0:NCB], -1.0, None,
                                            ALU.mult).then_inc(mean_made, 1)
                    dve.wait_ge(mean_made, 1)
                    nc.vector.tensor_tensor(gn_dev[:], gn_chan[:, :, 0], gn_mean[:],
                                            ALU.add).then_inc(mean_made, 1)
                    dve.wait_ge(mean_made, 2)
                    for cb in range(NCB):
                        nc.vector.scalar_tensor_tensor(
                            gn_sum[:, cb:cb + 1], gn_dev[:, cb:cb + 1], gn_dev[:, cb:cb + 1],
                            gn_chan[:, cb, 1:2], ALU.mult, ALU.add).then_inc(sq_made, 1)
                    dve.wait_ge(rstd_made, 1)
                    nc.vector.tensor_tensor(gn_bias[:], gn_mean[:], gn_rstd[:],
                                            ALU.mult).then_inc(bias_made, 1)
                    dve.wait_ge(w_ready, weights)
                    nc.vector.memset(ln_eps[:], LN_EPS[l]).then_inc(dve_own, 1)
                    dv = vec[:, V_D:V_D + K * NDB].rearrange("p (k d) -> p d k", k=K)
                    nc.vector.tensor_reduce(dsum[:], dv, AX.X, ALU.add).then_inc(dve_own, 1)
                    if last:
                        dve.wait_ge(dve_own, 2)
                        nc.vector.tensor_scalar(dsum[:], dsum[:], 1.0 / K, None, ALU.mult)
                    else:
                        al = vec[:, V_ALOG:V_ALOG + K * NDB * NS]
                        av = a_neg[:].rearrange("p k d n -> p (k d n)")
                        nc.vector.tensor_scalar(av, al, MAX_LOG, None, ALU.min).then_inc(dve_own, 1)
                    v = pad[:].rearrange("p d (h w) -> p d h w", w=PW)
                    if conv:
                        dve.wait_ge(border, 4)
                    with dve.Fori(0, NCH // 2) as j:
                        for q in range(2):
                            c = j * 2 + q
                            dve.wait_ge(in_mm, XN_FREE + c + 1)
                            src = ps[:, 3 * q:3 * q + NDB, :]
                            if conv:
                                src = src.rearrange("p d (r w) -> p d r w", w=W)
                                dst = v[:, :, bass.ds(c * RW + 1, RW), 1:1 + W]
                            else:
                                dst = u[:, :, bass.ds(c * T, T)]
                            nc.vector.tensor_copy(dst, src).then_inc(pad_made, 1)
                    if not last:
                        dve.wait_ge(a_made, 1)
                        nc.vector.tensor_scalar(av, av, -1.0, None, ALU.mult)
                    if not conv:
                        return
                    dve.wait_ge(pad_made, PAD_FREE + NCH)
                    with dve.Fori(0, NCH // 2) as j:
                        for q in range(2):
                            c = j * 2 + q
                            for s in range(DT_TAPS):
                                tap = PE_TAPS + s
                                for d in range(NDB):
                                    dst = cv[:, q, d, :].rearrange("p (r w) -> p r w", w=W)
                                    src = v[:, d, bass.ds(c * RW + tap // 3, RW),
                                            tap % 3:tap % 3 + W]
                                    wt = vec[:, V_TAP + d * TAPS + tap:V_TAP + d * TAPS + tap + 1]
                                    if s == 0:
                                        dve.wait_ge(cv_mm, c * NDB + d + 1)
                                        dve.wait_ge(cv_used, c * NDB + d + 1)
                                        part = ps[:, 3 * q + d, :].rearrange("p (r w) -> p r w", w=W)
                                    else:
                                        dve.wait_ge(cv_step, STEP_FREE + c * NDB * DT_TAPS
                                                    + NDB * (s - 1) + d + 1)
                                        part = dst
                                    nc.vector.scalar_tensor_tensor(
                                        dst, src, wt, part, ALU.mult, ALU.add).then_inc(cv_step, 1)

                @block.scalar
                def _(act):
                    if conv:
                        act.sem_inc(cv_used, CV_FREE)
                    nc.scalar.preload_act_table_set("natural_log_exp_and_others")
                    act.wait_ge(var_mm, 1)
                    nc.scalar.activation(gn_rstd[:], ps[0:CB, 6, 0:NCB], ACT.Ln,
                                         bias=gn_eps[:]).then_inc(act_own, 1)
                    act.wait_ge(act_own, 1)
                    nc.scalar.activation(gn_rstd[:], gn_rstd[:], ACT.Exp,
                                         scale=-0.5).then_inc(rstd_made, 1)
                    act.wait_ge(bias_made, 1)
                    with act.Fori(0, NCH // 2) as j:
                        for q in range(2):
                            c = j * 2 + q
                            act.wait_ge(in_mm, c + 1)
                            for cb in range(NCB):
                                nc.scalar.activation(xn[:, q, cb, :], xT[:, cb, bass.ds(c * T, T)],
                                                     ACT.Identity, bias=gn_bias[:, cb:cb + 1],
                                                     scale=gn_rstd[:, cb:cb + 1]).then_inc(xn_made, 1)
                    if not last:
                        act.wait_ge(dve_own, 3)
                        av = a_neg[:].rearrange("p k d n -> p (k d n)")
                        nc.scalar.activation(av, av, ACT.Exp).then_inc(a_made, 1)
                    if not conv:
                        return
                    nc.scalar.preload_act_table_set("silu_and_others")
                    act.wait_ge(w_ready, weights)
                    for tap in range(PE_TAPS):
                        for d in range(NDB):
                            j = V_TAP + d * TAPS + tap
                            nc.scalar.activation(tap_w[:, tap, d, :], ident[:], ACT.Copy,
                                                 scale=vec[:, j:j + 1]).then_inc(tap_made, 1)
                    with act.Fori(0, NCH // 2) as j:
                        for q in range(2):
                            c = j * 2 + q
                            for d in range(NDB):
                                act.wait_ge(cv_step, STEP_FREE + c * NDB * DT_TAPS
                                            + NDB * (DT_TAPS - 1) + d + 1)
                                nc.scalar.activation(u[:, d, bass.ds(c * T, T)], cv[:, q, d, :],
                                                     ACT.Silu, bias=vec[:, V_CB + d:V_CB + d + 1]
                                                     ).then_inc(cv_used, 1)

                @block.tensor
                def _(pe):
                    pe.sem_inc(in_mm, XN_FREE)
                    pe.wait_ge(sum_made, NCB)
                    nc.tensor.matmul(ps[0:CB, 6, 0:NCB], group_mean[:], gn_chan[:, :, 0],
                                     start=True, stop=True).then_inc(sum_mm, 1)
                    pe.wait_ge(mean_made, 1)
                    pe.wait_ge(sq_made, NCB)
                    nc.tensor.matmul(ps[0:CB, 6, 0:NCB], group_mean[:], gn_sum[:],
                                     start=True, stop=True).then_inc(var_mm, 1)
                    pe.wait_ge(in_loaded, 16)
                    with pe.Fori(0, NCH // 2) as j:
                        for q in range(2):
                            c = j * 2 + q
                            pe.wait_ge(xn_made, c * NCB + NCB)
                            pe.wait_ge(pad_made, c + 1)
                            for d in range(NDB):
                                for cb in range(NCB):
                                    last_mm = nc.tensor.matmul(
                                        ps[:, 3 * q + d, :], in_w[:, cb, d * P:(d + 1) * P],
                                        xn[:, q, cb, :], start=cb == 0, stop=cb == NCB - 1)
                            last_mm.then_inc(in_mm, 1)
                    if not conv:
                        return
                    v = pad[:].rearrange("p d (h w) -> p d h w", w=PW)
                    pe.wait_ge(tap_made, PE_TAPS * NDB)
                    pe.wait_ge(border, 4)
                    pe.wait_ge(pad_made, PAD_FREE + NCH)
                    with pe.Fori(0, NCH // 2) as j:
                        for q in range(2):
                            c = j * 2 + q
                            for d in range(NDB):
                                pe.wait_ge(cv_step, c * NDB * DT_TAPS + d + 1)
                                for tap in range(PE_TAPS):
                                    last_mm = nc.tensor.matmul(
                                        ps[:, 3 * q + d, :].rearrange("p (r w) -> p r w", w=W),
                                        tap_w[:, tap, d, :],
                                        v[:, d, bass.ds(c * RW + tap // 3, RW), tap % 3:tap % 3 + W],
                                        start=tap == 0, stop=tap == PE_TAPS - 1)
                                last_mm.then_inc(cv_mm, 1)
            nc.all_engine_barrier(sems_to_clear=all_sems)

        def scan(l):
            R = RANK[l]
            M = R + 2 * NS
            (bc_q0, bc_q1, dts_loaded, padded, xd_mm, xd_copied, xd_pre, xd_stored, z_mm, z_read,
             sp_abs, sp_exp, sp_ready, sp_half, dt_made, dtu_made, b_made, a_made, scanned,
             carried, g_made, y_mm, y_kept, xw_loaded, dw_loaded) = sems[:25]
            bc_loaded = (bc_q0, bc_q1)
            Y_BANK, X_BANK = 4, 7
            PADS = 4
            PRE_FREE = 2
            COPIED = PRE_FREE + NCH
            PE_Z = 0
            ACT_SP = (3, 5, 7)
            DVE_SP = (5, 7, 9)
            POOL_SP = (None, 8, 10)
            PE_XD, ACT_XD = 5, 10
            PE_Y = 3 * NDB
            ACT_Y = (2, 3, 4)

            def chunk(k, n, half):
                return k, n, half, k * NCH + n

            def chunks(eng, step):
                for k in range(K):
                    before = chunk(k - 1, NCH - 1, NCH // 2 - 1) if k else None
                    after = chunk(k + 1, 0, 0) if k + 1 < K else None
                    step(chunk(k, 0, 0), before, chunk(k, 1, 0), 0)
                    with eng.Fori(0, NCH // 2 - 1) as j:
                        c = [chunk(k, j * 2 + i, j + i // 2) for i in range(4)]
                        step(c[1], c[0], c[2], 1)
                        step(c[2], c[1], c[3], 0)
                    step(chunk(k, NCH - 1, NCH // 2 - 1), chunk(k, NCH - 2, NCH // 2 - 1), after, 1)

            def xd_of(k, n):
                return xd_dram[l][k][bass.ds(n, 1)].rearrange("o m t -> (o m) t")

            def make_dtu(eng, c, d, par):
                k, n, _, S = c
                eng.wait_ge(dt_made, S * NDB + d + 1)
                eng.tensor_tensor(as_chunk(dtu[:, par, d, :], k), as_chunk(dt[:, par, d, :], k),
                                  in_order(u, k, d, n), ALU.mult).then_inc(dtu_made, 1)

            with nc.Block(no_gpsimd_drain=True) as block:
                @block.sync
                def _(sp):
                    def load_dts(c):
                        k, n, _, S = c
                        wait(sp, z_mm, NDB * S)
                        sp.dma_start(dts[0:R], xd_of(k, n)[0:R]).then_inc(dts_loaded, 16)

                    sp.sem_inc(xd_pre, 16 * PRE_FREE)
                    for n in range(NCH):
                        sp.wait_ge(xd_copied, PRE_FREE + n + 1)
                        sp.wait_ge(xd_pre, (PRE_FREE + n) * 16)
                        sp.dma_start(xd_of(0, n), xd_sb2[0:M, n % 2, :]).then_inc(xd_pre, 16)
                    sp.wait_ge(xd_pre, (PRE_FREE + NCH) * 16)
                    load_dts(chunk(0, 0, 0))

                    def step(this, before, after, par):
                        k, n, _, S = this
                        if isinstance(n, int) and n == 0 and 0 < k < K - 1:
                            sp.wait_ge(xd_mm, k * NCH + NCH)
                            sp.dma_start(xp_w[:, (k + 1) % 2, :, 0:M], w_xp[l][:, k + 1]
                                         ).then_inc(xw_loaded, 16)
                            sp.wait_ge(z_mm, NDB * k * NCH)
                            sp.dma_start(dt_w[0:R, (k + 1) % 2], w_dt[l][:, k + 1]
                                         ).then_inc(dw_loaded, 16)
                        if after:
                            if after[0]:
                                sp.wait_ge(xd_stored, (after[3] - NCH + 1) * 16)
                            load_dts(after)
                        for g in range(NG):
                            wait(sp, b_made, (S * NG + g - 1) * NDB)
                            wait(sp, g_made, (S * NG + g - 1) * NDB)
                            src = xd_of(k, n)[R:M].rearrange("(b g n) t -> g b n t", b=2, g=NG)[g]
                            for b in range(2):
                                sp.dma_start(bc[:, g % 2, b], src[b].partition_broadcast(P)
                                             ).then_inc(bc_loaded[g % 2], 16)
                    chunks(sp, step)

                @block.tensor
                def _(pe):
                    def project_x(k, n, bank):
                        if k > 1:
                            pe.wait_ge(xw_loaded, (k - 1) * 16)
                        for d in range(NDB):
                            mm = nc.tensor.matmul(as_chunk(ps[0:M, bank, :], k),
                                                  xp_w[:, k % 2, d, 0:M], in_order(u, k, d, n),
                                                  start=d == 0, stop=d == NDB - 1)
                        mm.then_inc(xd_mm, 1)

                    def project_dt(c, d):
                        k, n, half, S = c
                        wait(pe, z_read, (S - 1) * NDB + d + 1)
                        if d == 0:
                            if k > 1:
                                pe.wait_ge(dw_loaded, (k - 1) * 16)
                            pe.wait_ge(dts_loaded, (S + 1) * 16)
                        nc.tensor.matmul(ps[:, d, :], dt_w[0:R, k % 2, d * P:(d + 1) * P],
                                         dts[0:R], start=True, stop=True).then_inc(z_mm, 1)

                    with pe.Fori(0, NCH // 2) as j:
                        for q in range(2):
                            n = j * 2 + q
                            pe.wait_ge(xd_copied, n + 1)
                            project_x(0, n, 3 + 4 * q)
                    for d in range(NDB):
                        project_dt(chunk(0, 0, 0), d)

                    def step(this, before, after, par):
                        k, n, _, S = this
                        for i in range(ITEMS):
                            g, d = divmod(i, NDB)
                            if after and i == PE_Z:
                                for dn in range(NDB):
                                    project_dt(after, dn)
                            if i == PE_XD and k + 1 < K:
                                pe.wait_ge(xd_copied, S + COPIED)
                                project_x(k + 1, n, X_BANK)
                            if g == 0:
                                wait(pe, y_kept, (S - 1) * NDB + d + 1)
                            if i - d == PE_Y:
                                if k == 0:
                                    w, src = skip_w[:, d, :], u
                                else:
                                    w, src = ident[:], y_acc
                                    pe.wait_ge(y_kept, S * NDB)
                                nc.tensor.matmul(as_chunk(ps[:, Y_BANK + d, :], k), w,
                                                 in_order(src, k, d, n), start=False, stop=False)
                            pe.wait_ge(g_made, S * ITEMS + i + 1)
                            for s in range(SG):
                                mm = nc.tensor.matmul(ps[:, Y_BANK + d, :], ident[:],
                                                      ring[:, i % RING, s, runs],
                                                      start=g == 0 and s == 0,
                                                      stop=g == NG - 1 and s == SG - 1)
                            mm.then_inc(y_mm, 1)
                    chunks(pe, step)

                @block.scalar
                def _(act):
                    def softplus(c, d, part, par):
                        k, n, _, S = c
                        t = sp_t[:, (par + d) % 2]
                        bias = vec[:, V_DTB + k * NDB + d:V_DTB + k * NDB + d + 1]
                        z = S * NDB + d
                        if part == 0:
                            act.wait_ge(z_mm, z + 1)
                            wait(act, dt_made, z - 1)
                            if d == 0:
                                wait(act, xd_stored, ((K - 1) * NCH if k == K - 1 and not (
                                    isinstance(n, int) and n == 0) else S - 1) * 16)
                            nc.scalar.activation(t[:, 0, :], ps[:, d, :], ACT.Abs,
                                                 bias=bias).then_inc(sp_abs, 1)
                            nc.scalar.activation(dt[:, par, d, :], ps[:, d, :], ACT.Relu,
                                                 bias=bias).then_inc(z_read, 1)
                        elif part == 1:
                            act.wait_ge(sp_abs, z + 1)
                            nc.scalar.activation(t[:, 0, :], t[:, 0, :], ACT.Exp,
                                                 scale=-1.0).then_inc(sp_exp, 1)
                        else:
                            act.wait_ge(sp_exp, z + 1)
                            nc.scalar.activation(t[:, 1, :], t[:, 0, :], ACT.Ln,
                                                 bias=1.0).then_inc(sp_ready, 1)

                    def keep_last(c, i):
                        g, d = divmod(i, NDB)
                        act.wait_ge(padded, PADS + c[3] * ITEMS + i + 1)
                        nc.scalar.activation(carry[:, d, g * SG:(g + 1) * SG],
                                             ring[:, i % RING, :, T if c[0] < 2 else 1],
                                             ACT.Copy).then_inc(carried, 1)

                    def start_runs(c, i):
                        k, n, _, S = c
                        g, d = divmod(i, NDB)
                        if isinstance(n, int) and n == 0:
                            if S == 0 and i == 0:
                                act.wait_ge(padded, PADS)
                            last = decays[:, i % 2, :, 0]
                        else:
                            act.wait_ge(carried, (S - 1) * ITEMS + i + 1)
                            last = carry[:, d, g * SG:(g + 1) * SG]
                        nc.scalar.activation(ring[:, i % RING, :, 0 if k < 2 else TP - 1], last,
                                             ACT.Copy).then_inc(padded, 1)

                    def keep_y(c, d):
                        k, n, _, S = c
                        act.wait_ge(y_mm, S * ITEMS + ITEMS - NDB + d + 1)
                        nc.scalar.activation(in_order(y_acc, k, d, n),
                                             as_chunk(ps[:, Y_BANK + d, :], k),
                                             ACT.Copy).then_inc(y_kept, 1)

                    nc.scalar.preload_act_table_set("natural_log_exp_and_others")
                    act.sem_inc(xd_copied, PRE_FREE)
                    for d in range(NDB):
                        nc.scalar.activation(skip_w[:, d, :], ident[:], ACT.Copy,
                                             scale=dsum[:, d:d + 1])
                    with act.Fori(0, NCH // 2) as j:
                        for q in range(2):
                            n = j * 2 + q
                            act.wait_ge(xd_mm, n + 1)
                            act.wait_ge(xd_pre, (n + 1) * 16)
                            nc.scalar.activation(xd_sb2[0:M, q, :], ps[0:M, 3 + 4 * q, :],
                                                 ACT.Copy).then_inc(xd_copied, 1)
                    for d in range(NDB):
                        for part in range(3):
                            softplus(chunk(0, 0, 0), d, part, 0)

                    def step(this, before, after, par):
                        k, n, _, S = this
                        for i in range(ITEMS):
                            g, d = divmod(i, NDB)
                            if g == 0:
                                act.wait_ge(dt_made, S * NDB + d + 1)
                            wait(act, scanned, S * ITEMS + i - 1)
                            if i >= 2:
                                keep_last(this, i - 2)
                            elif before:
                                keep_last(before, i - 2 + ITEMS)
                            start_runs(this, i)
                            for s in range(SG):
                                nc.scalar.activation(
                                    decays[:, i % 2, s, runs], dt[:, par, d, :], ACT.Exp,
                                    scale=a_neg[:, k, d, g * SG + s:g * SG + s + 1]).then_inc(a_made, 1)
                            if before and i in ACT_Y:
                                keep_y(before, ACT_Y.index(i))
                            if after:
                                for dn, at in enumerate(ACT_SP):
                                    if i - at in range(3):
                                        softplus(after, dn, i - at, 1 - par)
                            if k + 1 < K and i == ACT_XD:
                                act.wait_ge(xd_mm, S + NCH + 1)
                                act.wait_ge(dt_made, (S + 1) * NDB + 2)
                                nc.scalar.activation(sp_t[0:M, par, 0, :], ps[0:M, X_BANK, :],
                                                     ACT.Copy).then_inc(xd_copied, 1)
                            if k + 1 < K and i == ACT_XD + 1:
                                act.wait_ge(xd_copied, S + COPIED + 1)
                                act.dma_start(xd_of(k + 1, n), sp_t[0:M, par, 0, :]).then_inc(xd_stored, 16)
                    chunks(act, step)
                    end = chunk(K - 1, NCH - 1, NCH // 2 - 1)
                    for i in (ITEMS - 2, ITEMS - 1):
                        act.wait_ge(scanned, end[3] * ITEMS + i + 1)
                        keep_last(end, i)
                    for d in range(NDB):
                        keep_y(end, d)

                @block.vector
                def _(dve):
                    def guard(c, d, par):
                        t = sp_t[:, (par + d) % 2]
                        dve.wait_ge(sp_ready, c[3] * NDB + d + 1)
                        nc.vector.scalar_tensor_tensor(t[:, 1, :], t[:, 1, :], LN_SLACK, t[:, 0, :],
                                                       ALU.add, ALU.min).then_inc(sp_half, 1)

                    def make_dt(c, d, par):
                        t = sp_t[:, (par + d) % 2]
                        dve.wait_ge(sp_half, c[3] * NDB + d + 1)
                        nc.vector.tensor_tensor(dt[:, par, d, :], t[:, 1, :], dt[:, par, d, :],
                                                ALU.add).then_inc(dt_made, 1)
                        if d == 0:
                            make_dtu(dve, c, 0, par)

                    def make_input(c, i, par):
                        g, d = divmod(i, NDB)
                        k, n, _, S = c
                        if g == 0:
                            dve.wait_ge(dtu_made, S * NDB + d + 1)
                        if d == 0:
                            dve.wait_ge(bc_loaded[g % 2], (S * 2 + g // 2 + 1) * 32)
                        wait(dve, y_mm, S * ITEMS + i - RING + 1)
                        nc.vector.tensor_tensor(
                            ring[:, i % RING, :, runs], dtu[:, par, d:d + 1, :].to_broadcast([P, SG, T]),
                            bc[:, g % 2, 0], ALU.mult).then_inc(b_made, 1)

                    for edge in (0, TP - 1):
                        nc.vector.memset(ring[:, :, :, edge], 0.0).then_inc(padded, 1)
                        nc.vector.memset(decays[:, :, :, edge], 0.0).then_inc(padded, 1)
                    for d in range(NDB):
                        guard(chunk(0, 0, 0), d, 0)
                        make_dt(chunk(0, 0, 0), d, 0)
                    make_input(chunk(0, 0, 0), 0, 0)

                    def step(this, before, after, par):
                        k, n, _, S = this
                        for i in range(ITEMS):
                            g, d = divmod(i, NDB)
                            dve.wait_ge(b_made, S * ITEMS + i + 1)
                            dve.wait_ge(padded, PADS + S * ITEMS + i + 1)
                            dve.wait_ge(a_made, (S * ITEMS + i + 1) * SG)
                            h = ring[:, i % RING].rearrange("p n t -> p (n t)")
                            decay = decays[:, i % 2].rearrange("p n t -> p (n t)")
                            if k >= 2:
                                h, decay = h[:, ::-1], decay[:, ::-1]
                            nc.vector.tensor_tensor_scan(h, decay, h, 0.0, ALU.mult,
                                                         ALU.add).then_inc(scanned, 1)
                            if i + 1 < ITEMS:
                                make_input(this, i + 1, par)
                            elif after:
                                make_input(after, 0, 1 - par)
                            if after:
                                for dn, at in enumerate(DVE_SP):
                                    if i == at:
                                        guard(after, dn, 1 - par)
                                    if i == at + 1:
                                        make_dt(after, dn, 1 - par)
                    chunks(dve, step)

                @block.gpsimd
                def _(pool):
                    for d in range(1, NDB):
                        make_dtu(pool, chunk(0, 0, 0), d, 0)

                    def step(this, before, after, par):
                        S = this[3]
                        for i in range(ITEMS):
                            g, d = divmod(i, NDB)
                            if d == 0:
                                pool.wait_ge(bc_loaded[g % 2], (S * 2 + g // 2 + 1) * 32)
                            pool.wait_ge(carried, S * ITEMS + i + 1)
                            nc.gpsimd.tensor_tensor(ring[:, i % RING, :, runs],
                                                    ring[:, i % RING, :, runs],
                                                    bc[:, g % 2, 1], ALU.mult).then_inc(g_made, 1)
                            if after and i in POOL_SP:
                                make_dtu(pool, after, POOL_SP.index(i), 1 - par)
                    chunks(pool, step)
            nc.all_engine_barrier(sems_to_clear=all_sems)

        def out_proj(l, b):
            last = l == 3
            (in_loaded, x_half0, x_half1, out_loaded, ys_half, ys_made, ss_half, ss_made,
             stats_made, x_out, xn_made, in_mm, z_made, y_made, mean_mm, yc_made, sq_made, var_mm,
             ln_made, rs_made, yn_made, aff_made, gate_made, out_mm, res_made) = sems[:25]
            XN_FREE, Z_FREE, YC_FREE, RES_FREE = 2, 2, 2, 2

            PAIRS = NCH // 2

            with nc.Block(no_gpsimd_drain=True) as block:
                @block.sync
                def _(sp):
                    if not last:
                        kept = image_of(x_in, b) if l == 0 else x_dram
                        sp.dma_start(in_w, w_in[l]).then_inc(in_loaded, 16)
                        for h, loaded in enumerate((x_half0, x_half1)):
                            at = slice(h * L // 2, (h + 1) * L // 2)
                            sp.dma_start(xT[:, :, at], kept[:, :, at]).then_inc(loaded, 16)
                        sp.dma_start(out_w, w_out[l]).then_inc(out_loaded, 16)
                        for loaded in (in_loaded, x_half0, x_half1, out_loaded):
                            sp.wait_ge(loaded, 16)
                    else:
                        sp.wait_ge(res_made, RES_FREE + NCH)
                        sp.dma_start(image_of(out, b), xT).then_inc(x_out, 16)
                        sp.wait_ge(x_out, 16)

                @block.tensor
                def _(pe):
                    pe.sem_inc(in_mm, XN_FREE)
                    if not last:
                        pe.wait_ge(in_loaded, 16)
                    with pe.Fori(0, NCH // 2) as j:
                        for q in range(2):
                            c = j * 2 + q
                            pe.wait_ge(xn_made, c * NCB + NCB)
                            pe.wait_ge(z_made, c + 1)
                            for d in range(NDB):
                                for cb in range(NCB):
                                    mm = nc.tensor.matmul(
                                        ps[:, 3 * q + d, :], in_w[:, cb, DI + d * P:DI + (d + 1) * P],
                                        xn[:, q, cb, :], start=cb == 0, stop=cb == NCB - 1)
                            mm.then_inc(in_mm, 1)
                    pe.wait_ge(z_made, Z_FREE + NCH)
                    if not last:
                        pe.wait_ge(out_loaded, 16)

                    def mean_of(c, q):
                        pe.wait_ge(yc_made, c + 1)
                        pe.wait_ge(ys_made, c + 1)
                        nc.tensor.matmul(ps[:, q, :], chan_mean[:], y_sum[:, q, :],
                                         start=True, stop=True).then_inc(mean_mm, 1)

                    pe.sem_inc(yc_made, YC_FREE)
                    def variance(p):
                        for q in range(2):
                            pe.wait_ge(ss_made, 2 * p + q + 1)
                            wait(pe, ln_made, 2 * p + q - 1)
                            nc.tensor.matmul(ps[:, 2 + q, :], chan_mean[:], sq_sum[:, q, :],
                                             start=True, stop=True).then_inc(var_mm, 1)

                    for c in range(4):
                        mean_of(c, c % 2)
                        if c == 1:
                            variance(0)
                    for p in range(PAIRS):
                        if p + 1 < PAIRS:
                            variance(p + 1)
                        for q in range(2):
                            c = 2 * p + q
                            if q == 1 and p + 2 < PAIRS:
                                mean_of(c + 3, 0)
                                mean_of(c + 4, 1)
                            if last:
                                pe.wait_ge(aff_made, c * NDB + NDB)
                            else:
                                pe.wait_ge(gate_made, c + 1)
                            pe.wait_ge(res_made, c + 1)
                            for cb in range(NCB):
                                for d in range(NDB):
                                    mm = nc.tensor.matmul(
                                        ps[0:CB, 4 + 2 * q + cb, :], out_w[:, d, cb * CB:(cb + 1) * CB],
                                        yc[:, c % 4, d, :], start=d == 0, stop=d == NDB - 1)
                            mm.then_inc(out_mm, 1)

                @block.scalar
                def _(act):
                    def normalise(c, q):
                        act.wait_ge(in_mm, c + 1)
                        for cb in range(NCB):
                            nc.scalar.activation(xn[:, q, cb, :], xT[:, cb, bass.ds(c * T, T)],
                                                 ACT.Identity, bias=gn_bias[:, cb:cb + 1],
                                                 scale=gn_rstd[:, cb:cb + 1]).then_inc(xn_made, 1)

                    def silu(c, q):
                        act.wait_ge(in_mm, XN_FREE + c + 1)
                        if last:
                            wait(act, y_made, (c - 1) * NDB)
                            dst = sq[:, q]
                        else:
                            dst = u[:, :, bass.ds(c * T, T)]
                        nc.scalar.activation(dst, ps[:, 3 * q:3 * q + NDB, :],
                                             ACT.Silu).then_inc(z_made, 1)

                    act.sem_inc(z_made, Z_FREE)
                    if not last:
                        act.wait_ge(x_half0, 16)
                    nc.scalar.preload_act_table_set("silu_and_others")
                    for q in range(2):
                        normalise(q, q)
                    silu(0, 0)
                    normalise(2, 0)
                    if not last:
                        act.wait_ge(x_half1, 16)
                    with act.Fori(0, NCH // 2 - 2) as j:
                        for q in range(2):
                            c = j * 2 + q + 1
                            silu(c, 1 - q)
                            normalise(c + 2, 1 - q)
                    silu(NCH - 3, 1)
                    normalise(NCH - 1, 1)
                    silu(NCH - 2, 0)
                    silu(NCH - 1, 1)
                    nc.scalar.preload_act_table_set("natural_log_exp_and_others")

                    def squares(p):
                        for q in range(2):
                            c = 2 * p + q
                            act.wait_ge(yc_made, YC_FREE + c + 1)
                            wait(act, ss_made, c - 1)
                            nc.scalar.activation(sq[:, q], yc[:, c % 4], ACT.Square).then_inc(sq_made, 1)

                    def normalise_y(p):
                        for q in range(2):
                            c = 2 * p + q
                            act.wait_ge(var_mm, c + 1)
                            wait(act, yn_made, c - 1)
                            nc.scalar.activation(rs[:, q, :], ps[:, 2 + q, :], ACT.Ln,
                                                 bias=ln_eps[:]).then_inc(ln_made, 1)
                            act.wait_ge(ln_made, c + 1)
                            nc.scalar.activation(rs[:, q, :], rs[:, q, :], ACT.Exp,
                                                 scale=-0.5).then_inc(rs_made, 1)
                        for q in range(2):
                            c = 2 * p + q
                            act.wait_ge(yn_made, c + 1)
                            for d in range(NDB):
                                nc.scalar.activation(yc[:, c % 4, d, :], yc[:, c % 4, d, :],
                                                     ACT.Identity,
                                                     bias=vec[:, V_LNB + d:V_LNB + d + 1],
                                                     scale=vec[:, V_LNW + d:V_LNW + d + 1]
                                                     ).then_inc(aff_made, 1)

                    squares(0)
                    squares(1)
                    normalise_y(0)
                    for p in range(PAIRS - 1):
                        normalise_y(p + 1)
                        if p + 2 < PAIRS:
                            squares(p + 2)

                @block.vector
                def _(dve):
                    if last:
                        with dve.Fori(0, NCH // 2) as j:
                            for q in range(2):
                                c = j * 2 + q
                                dve.wait_ge(z_made, Z_FREE + c + 1)
                                for d in range(NDB):
                                    nc.vector.scalar_tensor_tensor(
                                        y_acc[:, d, bass.ds(c * T, T)], u[:, d, bass.ds(c * T, T)],
                                        dsum[:, d:d + 1], sq[:, q, d, :], ALU.mult,
                                        ALU.mult).then_inc(y_made, 1)
                    dve.sem_inc(res_made, RES_FREE)
                    if last:
                        dve.wait_ge(y_made, NCH * NDB)
                    else:
                        dve.wait_ge(x_half0, 16)
                        dve.wait_ge(x_half1, 16)

                    def sum_y(c, q):
                        y = y_acc[:, :, bass.ds(c * T, T)]
                        nc.vector.tensor_tensor(y_sum[:, q, :], y[:, 0], y[:, 1],
                                                ALU.add).then_inc(ys_half, 1)
                        dve.wait_ge(ys_half, c + 1)
                        nc.vector.tensor_tensor(y_sum[:, q, :], y_sum[:, q, :], y[:, 2],
                                                ALU.add).then_inc(ys_made, 1)

                    def centre(c, y):
                        dve.wait_ge(mean_mm, c + 1)
                        wait(dve, out_mm, c - 3)
                        nc.vector.tensor_tensor(
                            yc[:, y], y_acc[:, :, bass.ds(c * T, T)],
                            ps[:, y % 2:y % 2 + 1, :].to_broadcast([P, NDB, T]),
                            ALU.subtract).then_inc(yc_made, 1)

                    def scale_y(p):
                        for q in range(2):
                            c = 2 * p + q
                            dve.wait_ge(rs_made, c + 1)
                            nc.vector.tensor_tensor(
                                yc[:, c % 4], yc[:, c % 4], rs[:, q:q + 1, :].to_broadcast([P, NDB, T]),
                                ALU.mult).then_inc(yn_made, 1)

                    for p in range(2):
                        for c in (2 * p, 2 * p + 1):
                            sum_y(c, c % 2)
                        for c in (2 * p, 2 * p + 1):
                            centre(c, c)
                    scale_y(0)
                    for p in range(PAIRS):
                        if p + 2 < PAIRS:
                            for q in range(2):
                                sum_y(2 * p + 4 + q, q)
                        if p + 1 < PAIRS:
                            scale_y(p + 1)
                        for q in range(2):
                            c = 2 * p + q
                            dve.wait_ge(out_mm, c + 1)
                            xc = xT[:, :, bass.ds(c * T, T)]
                            nc.vector.tensor_tensor(xc, xc, ps[0:CB, 4 + 2 * q:6 + 2 * q, :],
                                                    ALU.add).then_inc(res_made, 1)
                            if p + 2 < PAIRS:
                                centre(c + 4, c % 4)
                            if not last:
                                dve.wait_ge(res_made, RES_FREE + c + 1)
                                chunk_stats(c, stats_made)

                @block.gpsimd
                def _(pool):
                    if not last:
                        pool.wait_ge(z_made, Z_FREE + NCH)

                    def sum_squares(p):
                        for q in range(2):
                            c = 2 * p + q
                            pool.wait_ge(sq_made, c + 1)
                            wait(pool, var_mm, c - 1)
                            nc.gpsimd.tensor_tensor(sq_sum[:, q, :], sq[:, q, 0, :], sq[:, q, 1, :],
                                                    ALU.add).then_inc(ss_half, 1)
                            pool.wait_ge(ss_half, c + 1)
                            nc.gpsimd.tensor_tensor(sq_sum[:, q, :], sq_sum[:, q, :], sq[:, q, 2, :],
                                                    ALU.add).then_inc(ss_made, 1)

                    sum_squares(0)
                    sum_squares(1)
                    def gate(p):
                        for c in (2 * p, 2 * p + 1):
                            pool.wait_ge(aff_made, c * NDB + NDB)
                            nc.gpsimd.tensor_tensor(yc[:, c % 4], yc[:, c % 4],
                                                    u[:, :, bass.ds(c * T, T)],
                                                    ALU.mult).then_inc(gate_made, 1)

                    if not last:
                        gate(0)
                    for p in range(PAIRS - 1):
                        if not last:
                            gate(p + 1)
                        if p + 2 < PAIRS:
                            sum_squares(p + 2)
            nc.all_engine_barrier(sems_to_clear=all_sems)

        with nc.Fori(0, IMAGES) as b:
            for l in range(4):
                norm_conv(l, b)
                if l < 3:
                    scan(l)
                out_proj(l, b)


def _blocks(a, blocks, axis):
    s = a.shape
    a = a.reshape(s[:axis] + (blocks, s[axis] // blocks) + s[axis + 1:])
    return np.ascontiguousarray(np.moveaxis(a, axis + 1, 0))


def kernel(**inputs):
    import concourse.bacc as bacc
    from concourse.bass_utils import run_bass_kernel_spmd

    a = {name: np.asarray(value) for name, value in inputs.items()}
    names = (
        dict(i="in_proj_weight", o="out_proj_weight", x="x_proj_weight", t="dt_projs_weight",
             tb="dt_projs_bias", w="out_norm_weight", b="out_norm_bias"),
        dict(i="in_proj_w", o="out_proj_w", x="x_proj_w", t="dt_w", tb="dt_bias", w="ln_w", b="ln_b"),
        dict(i="in_proj_w", o="out_proj_w", x="x_proj_weight", t="dt_projs_weight",
             tb="dt_projs_bias", w="ln_gamma", b="ln_beta"),
        dict(i="in_proj_w", o="out_proj_w", x="x_proj_weight", t="dt_projs_weight",
             tb="dt_projs_bias", w="ln_gamma", b="ln_beta"),
    )
    arrays = {
        "x": np.ascontiguousarray(
            a["x"].reshape(-1, L, NCB, CB).transpose(0, 3, 2, 1))[:IMAGES],
        "ident": np.eye(P, dtype=np.float32),
        "group_mean": np.kron(np.eye(CB * GROUPS // DM), np.full((DM // GROUPS,) * 2,
                              GROUPS / DM)).astype(np.float32),
        "chan_mean": np.full((P, P), 1.0 / DI, np.float32),
    }
    zeros = np.zeros
    for l, n in enumerate(names):
        def of(key):
            return a[f"L{l}_conv_{key}"]
        arrays[f"w_in{l}"] = _blocks(of(n["i"]).T, NCB, 0)
        arrays[f"w_out{l}"] = _blocks(of(n["o"]).T, NDB, 0)
        if l < 3:
            arrays[f"w_xp{l}"] = np.ascontiguousarray(
                _blocks(of(n["x"]), NDB, 2).transpose(0, 1, 3, 2))
            arrays[f"w_dt{l}"] = np.ascontiguousarray(of(n["t"]).transpose(2, 0, 1))
            skip = _blocks(of("Ds").reshape(K, DI), NDB, 1)
        else:
            skip = _blocks(of("Ds").reshape(DI, K).T, NDB, 1)
        if l == 0:
            taps, cb = zeros((P, NDB, TAPS), np.float32), zeros((P, NDB), np.float32)
        else:
            cw = of("conv_w").reshape(TAPS, DI).T if l == 3 else of("conv_w").reshape(DI, TAPS)
            taps, cb = _blocks(cw, NDB, 0), _blocks(of("conv_b"), NDB, 0)
        parts = (_blocks(of(n["tb"]), NDB, 1), skip, _blocks(of("A_logs").reshape(K, DI, NS), NDB, 1),
                 _blocks(of(n["w"]), NDB, 0), _blocks(of(n["b"]), NDB, 0), cb, taps)
        arrays[f"vec{l}"] = np.ascontiguousarray(
            np.concatenate([p.reshape(P, -1) for p in parts], axis=1))

    nc = bacc.Bacc("TRN2", target_bir_lowering=False, num_devices=1,
                   dynamic_dma_scratch_size=1024)
    ap = {name: nc.dram_tensor(name + "_in", v.shape, mybir.dt.from_np(v.dtype),
                               kind="ExternalInput").ap() for name, v in arrays.items()}
    out = nc.dram_tensor("x_out", (IMAGES, CB, NCB, L), F32, kind="ExternalOutput").ap()
    build(nc, ap["x"], ap["ident"], ap["group_mean"], ap["chan_mean"],
          [ap[f"w_in{l}"] for l in range(4)], [ap[f"w_out{l}"] for l in range(4)],
          [ap[f"w_xp{l}"] for l in range(3)], [ap[f"w_dt{l}"] for l in range(3)],
          [ap[f"vec{l}"] for l in range(4)], out)
    r = run_bass_kernel_spmd(nc, [{name + "_in": v for name, v in arrays.items()}], core_ids=[0])
    got = np.asarray(r.results[0]["x_out"])
    return np.ascontiguousarray(got.transpose(0, 3, 2, 1)).reshape(IMAGES, H, W, DM)
```
